# Optimizing a Trainium2 kernel written in Bass

```python
import numpy as np
import jax
import jax.numpy as jnp

def _softmax(x, axis=-1):
    return jax.nn.softmax(x, axis=axis)

def _gelu(x):
    return jax.nn.gelu(x, approximate=True)

def _silu(x):
    return jax.nn.silu(x)

def _sigmoid(x):
    return jax.nn.sigmoid(x)

def _layernorm(x, axis=-1, eps=1e-05):
    m = jnp.mean(x, axis=axis, keepdims=True)
    v = jnp.var(x, axis=axis, keepdims=True)
    return (x - m) / jnp.sqrt(v + eps)

def _scatter_add(tgt, idx, src, axis=0):
    return tgt.at[idx].add(src)

def _segment_sum(src, seg, n):
    return jax.ops.segment_sum(src, seg, n)
kernel_name = 'mk_sandwich_d1_jaxref_r4_0ae248'

def setup_inputs(seed: int=0):
    np.random.seed(seed)
    _w = jnp.asarray

    def _L0_attn_setup():
        import jax, jax.numpy as jnp
        import numpy as np
        B, S, D = (4, 512, 256)
        H, K = (16, 64)
        EPS = 0.001
        key = jax.random.key(seed)
        ks = jax.random.split(key, 11)
        s = 0.02
        return {'x': jax.random.normal(ks[0], (B, S, D), jnp.float32), 'Wq': jax.random.normal(ks[1], (D, H, K), jnp.float32) * s, 'bq': jnp.zeros((H, K), jnp.float32), 'Wk': jax.random.normal(ks[2], (D, H, K), jnp.float32) * s, 'bk': jnp.zeros((H, K), jnp.float32), 'Wv': jax.random.normal(ks[3], (D, H, K), jnp.float32) * s, 'bv': jnp.zeros((H, K), jnp.float32), 'Wo': jax.random.normal(ks[4], (H, K, D), jnp.float32) * s, 'bo': jnp.zeros((D,), jnp.float32), 'gamma': jnp.ones((D,), jnp.float32), 'beta': jnp.zeros((D,), jnp.float32)}
    _L0_attn_in = _L0_attn_setup()

    def _L0_ffn_setup():
        import jax, jax.numpy as jnp
        import numpy as np
        DIM = 256
        HIDDEN = 768
        SCALE = 1.0 / 127.0

        def _dequant(w_int, dtype):
            return w_int.astype(dtype) * jnp.asarray(SCALE, dtype)
        key = jax.random.key(seed)
        k_x, k_g, k_u, k_d = jax.random.split(key, 4)
        x = jax.random.normal(k_x, (4, 512, DIM), dtype=jnp.float32)
        w_gate = jax.random.randint(k_g, (HIDDEN, DIM), -127, 128, dtype=jnp.int32)
        w_up = jax.random.randint(k_u, (HIDDEN, DIM), -127, 128, dtype=jnp.int32)
        w_down = jax.random.randint(k_d, (DIM, HIDDEN), -127, 128, dtype=jnp.int32)
        return {'x': x, 'w_gate': w_gate, 'w_up': w_up, 'w_down': w_down}
    _L0_ffn_in = _L0_ffn_setup()
    _d = {'L0_attn_x': _L0_attn_in['x'], 'L0_attn_Wq': _L0_attn_in['Wq'], 'L0_attn_bq': _L0_attn_in['bq'], 'L0_attn_Wk': _L0_attn_in['Wk'], 'L0_attn_bk': _L0_attn_in['bk'], 'L0_attn_Wv': _L0_attn_in['Wv'], 'L0_attn_bv': _L0_attn_in['bv'], 'L0_attn_Wo': _L0_attn_in['Wo'], 'L0_attn_bo': _L0_attn_in['bo'], 'L0_attn_gamma': _L0_attn_in['gamma'], 'L0_attn_beta': _L0_attn_in['beta'], 'L0_ffn_w_gate': _L0_ffn_in['w_gate'], 'L0_ffn_w_up': _L0_ffn_in['w_up'], 'L0_ffn_w_down': _L0_ffn_in['w_down']}
    _x0 = _d['L0_attn_x']
    _d['L0_attn_x'] = jax.random.normal(jax.random.fold_in(jax.random.key(seed), 1), (2, 2048, 256), dtype=_x0.dtype)
    del _x0
    return _d

def reference(L0_attn_x, L0_attn_Wq, L0_attn_bq, L0_attn_Wk, L0_attn_bk, L0_attn_Wv, L0_attn_bv, L0_attn_Wo, L0_attn_bo, L0_attn_gamma, L0_attn_beta, L0_ffn_w_gate, L0_ffn_w_up, L0_ffn_w_down):

    def _L0_attn_ref(x, Wq, bq, Wk, bk, Wv, bv, Wo, bo, gamma, beta):
        import jax, jax.numpy as jnp
        import numpy as np
        B, S, D = (4, 512, 256)
        H, K = (16, 64)
        EPS = 0.001
        q = jnp.einsum('bsd,dhk->bshk', x, Wq) + bq
        k = jnp.einsum('bsd,dhk->bshk', x, Wk) + bk
        v = jnp.einsum('bsd,dhk->bshk', x, Wv) + bv
        scale = 1.0 / jnp.sqrt(jnp.asarray(K, x.dtype))
        scores = jnp.einsum('bqhk,bshk->bhqs', q, k) * scale
        attn = jax.nn.softmax(scores, axis=-1)
        ctx = jnp.einsum('bhqs,bshk->bqhk', attn, v)
        attn_out = jnp.einsum('bqhk,hkd->bqd', ctx, Wo) + bo
        y = x + attn_out
        mu = jnp.mean(y, axis=-1, keepdims=True)
        var = jnp.mean(jnp.square(y - mu), axis=-1, keepdims=True)
        return (y - mu) * jax.lax.rsqrt(var + EPS) * gamma + beta

    def _L0_ffn_ref(x, w_gate, w_up, w_down):
        import jax, jax.numpy as jnp
        import numpy as np
        DIM = 256
        HIDDEN = 768
        SCALE = 1.0 / 127.0

        def _dequant(w_int, dtype):
            return w_int.astype(dtype) * jnp.asarray(SCALE, dtype)
        wg = _dequant(w_gate, x.dtype)
        wu = _dequant(w_up, x.dtype)
        wd = _dequant(w_down, x.dtype)
        gate = jnp.einsum('bsd,hd->bsh', x, wg)
        up = jnp.einsum('bsd,hd->bsh', x, wu)
        h = jax.nn.silu(gate) * up
        return jnp.einsum('bsh,dh->bsd', h, wd)
    x = L0_attn_x
    x = x + _layernorm(_L0_attn_ref(_layernorm(x, axis=-1), L0_attn_Wq, L0_attn_bq, L0_attn_Wk, L0_attn_bk, L0_attn_Wv, L0_attn_bv, L0_attn_Wo, L0_attn_bo, L0_attn_gamma, L0_attn_beta), axis=-1)
    x = x + _layernorm(_L0_ffn_ref(_layernorm(x, axis=-1), L0_ffn_w_gate, L0_ffn_w_up, L0_ffn_w_down), axis=-1)
    return x

_drawn_inputs = setup_inputs


def setup_inputs(seed=0):
    import zlib

    import numpy as np

    out = dict(_drawn_inputs(seed))
    spreads = {'L0_attn_bq': (0.0, 0.8),
     'L0_attn_bk': (0.0, 2.0),
     'L0_attn_bv': (0.0, 0.349),
     'L0_attn_bo': (0.0, 0.1),
     'L0_attn_gamma': (1.0, 0.2),
     'L0_attn_beta': (0.0, 0.1)}
    factors = {'L0_attn_Wq': 8.0, 'L0_attn_Wk': 8.0, 'L0_attn_Wv': 8.0}
    for name, (base, spread) in spreads.items():
        noise = np.random.default_rng([zlib.crc32(name.encode()), seed]).standard_normal(out[name].shape)
        drawn = base * np.exp(spread * noise) if base else spread * noise
        out[name] = jnp.asarray(drawn.astype(out[name].dtype))
    for name, factor in factors.items():
        out[name] = (out[name] * factor).astype(out[name].dtype)
    return out
```

```python
from contextlib import ExitStack

import concourse.bass as bass
from concourse import mybir

P = 128
ALU = mybir.AluOpType
ACT = mybir.ActivationFunctionType
F32 = mybir.dt.float32
F32R = mybir.dt.float32r
F16 = mybir.dt.float16
I32 = mybir.dt.int32
AX_X = mybir.AxisListType.X

EPS_LN = 1e-5
EPS_ATTN = 1e-3
BLK = 512
RING = 4
PROBS = 8
AHEAD = 6
LO_AHEAD = 3
P_SHIFT = 5.545177444479562
LO_SCALE = 2048.0
CHUNKS_AT = (3, 11)


def lo_on_dve(t):
    return t % 8 in (0, 2, 5)


def lo_counts(t):
    dve = sum(lo_on_dve(k) for k in range(t + 1))
    return dve, t + 1 - dve


NORM = 15
RSQRT_SEED = float(0x5F3759DF)


def norm(nc, dve, dst, src, eps, small, step, value):
    stats, mv, v, y, w = small
    tiles = dst.shape[1]
    n = [0]

    def then(ins):
        n[0] += 1
        ins.then_inc(step, 1)
        dve.wait_ge(step, value + n[0])

    for t in range(tiles):
        ins = nc.vector.bn_stats(stats[:, t], src[:, t])
    then(ins)
    nc.vector.memset(v[:, :], 0.0)
    for t in range(tiles):
        ins = nc.vector.bn_aggr(mv[:, t], stats[:, t])
    then(ins)
    then(nc.vector.tensor_scalar(v[:, :], mv[:, :, 1], eps, None, ALU.add))
    then(nc.vector.tensor_scalar(w[:, :].bitcast(I32), v[:, :].bitcast(I32), 1, None, ALU.logical_shift_right))
    then(nc.vector.tensor_scalar(y[:, :].bitcast(I32), w[:, :].bitcast(I32), -1.0, RSQRT_SEED, ALU.mult, ALU.add))
    for _ in range(3):
        then(nc.vector.tensor_tensor(w[:, :], y[:, :], y[:, :], ALU.mult))
        then(nc.vector.scalar_tensor_tensor(out=w[:, :], in0=w[:, :], scalar=-0.5, in1=v[:, :],
                                            op0=ALU.mult, op1=ALU.mult))
        then(nc.vector.scalar_tensor_tensor(out=y[:, :], in0=w[:, :], scalar=1.5, in1=y[:, :],
                                            op0=ALU.add, op1=ALU.mult))
    for t in range(tiles):
        ins = nc.vector.tensor_scalar(dst[:, t], src[:, t], mv[:, t, 0:1], y[:, t:t + 1], ALU.subtract, ALU.mult)
    then(ins)
    assert n[0] == NORM


def attention(nc, x, wqk, bqk, Wv, bv, ident_in, v_scratch, scratch):
    B, S, D = x.shape
    H = wqk.shape[1]
    K = wqk.shape[2] // 2
    DT = D // P
    KT = S // P
    NB = S // BLK
    TB = BLK // P
    STEPS = NB * KT
    AUX = NB + STEPS
    PRO_AUX = 2 * NB + 2 * KT
    PRO = NB * DT + KT * 2
    VW = 2 * K + 1
    DVE_LO, POOL_LO = lo_counts(STEPS - 1)
    HH = H // 2

    with ExitStack() as ctx:
        sb = lambda n, s, d: ctx.enter_context(nc.sbuf_tensor(n, s, d))
        sem = lambda n: ctx.enter_context(nc.semaphore(n))
        ps_score = ctx.enter_context(nc.psum_tensor("ps_score", [P, RING, BLK], F32))
        ps_aux = ctx.enter_context(nc.psum_tensor("ps_aux", [P, 2, BLK], F32))
        ps_ctx = ctx.enter_context(nc.psum_tensor("ps_ctx", [P, 2, BLK], F32))

        qA = [sb(f"q_hilo{u}", [P, S], F32R) for u in range(2)]
        kA = [sb(f"k_hihi{u}", [P, S], F32R) for u in range(2)]
        qB = [sb(f"q_hi_max{u}", [K + 1, S], F32R) for u in range(2)]
        kB = [sb(f"k_lo_one{u}", [K + 1, S], F32R) for u in range(2)]
        hi_st = sb("hi_st", [P, S], F32)
        lo_st = sb("lo_st", [P, S], F32)
        xTh = sb("xTh", [P, DT, S], F32R)
        xTl = sb("xTl", [P, DT, S], F32R)
        v_new = sb("v_new", [P, 2, HH, VW], F16)
        V = [sb(f"v_hi_one_lo{u}", [P, KT, VW], F16) for u in range(2)]
        p_f = sb("p_f", [P, PROBS, BLK], F32)
        p_h = sb("p_h", [P, PROBS, BLK], F16)
        p_l = sb("p_l", [P, PROBS, BLK], F16)
        w_raw = sb("w_raw", [P, DT, P], F32)
        w_h = sb("w_h", [P, DT, P], F32R)
        w_l = sb("w_l", [P, DT, P], F32R)
        bias = sb("bias", [P, H], F32)
        b_cur = sb("b_cur", [P, 1], F32)
        ident = sb("ident", [P, P], F32)
        mx = sb("mx", [P, 2, TB, NB], F32)
        mrow = sb("mrow", [P, 2, TB], F32)
        negm = sb("negm", [P, 2, TB], F32R)
        b_sum = sb("b_sum", [P, TB, K], F32)
        rden = sb("rden", [P, TB], F32)
        ctx_u = sb("ctx_u", [P, TB, K], F32)
        ctx_n = sb("ctx_n", [P, 2, TB, K], F32)
        stats = sb("stats", [P, TB, 6], F32)
        mv = sb("mv", [P, TB, 2], F32)
        small = (stats, mv, *(sb(f"norm{k}", [P, TB], F32) for k in range(3)))

        const_in = sem("const_in")
        ones_set = sem("ones_set")
        x_in = sem("x_in")
        ln_step = sem("ln_step")
        pro_full = sem("pro_full")
        pro_free = sem("pro_free")
        xh_ready = sem("xh_ready")
        wv_in = sem("wv_in")
        wvh_ready = sem("wvh_ready")
        wv_ready = sem("wv_ready")
        bv_in = sem("bv_in")
        vh_ready = sem("vh_ready")
        vd_ready = sem("vd_ready")
        v_ready = sem("v_ready")
        v_kept = [sem(f"v_kept{u}") for u in range(2)]
        v_full = [sem(f"v_full{u}") for u in range(2)]
        w_in = sem("w_in")
        wh_ready = sem("wh_ready")
        w_split = sem("w_split")
        aux_full = sem("aux_full")
        max_read = sem("max_read")
        hi_ready = sem("hi_ready")
        staged = sem("staged")
        slot_full = sem("slot_full")
        max_step = sem("max_step")
        negm_ready = sem("negm_ready")
        max_row = [sem(f"max_row{u}") for u in range(2)]
        s_full = sem("s_full")
        exp_done = sem("exp_done")
        lo_dve = sem("lo_dve")
        lo_pool = sem("lo_pool")
        pv_done = sem("pv_done")
        ev_step = sem("ev_step")
        ctx_free = sem("ctx_free")
        ctx_ready = sem("ctx_ready")
        ctx_out = [sem(f"ctx_out{u}") for u in range(2)]

        wvh_v = qA[1][:, :].rearrange("p (c n) -> p c n", c=DT)
        wvl_v = kA[1][:, :].rearrange("p (c n) -> p c n", c=DT)
        wv_raw = p_f[:, 0:4, :].rearrange("p r n -> p (r n)").rearrange("p (c n) -> p c n", c=DT)
        bv_all = p_f[:, 0:2, :].rearrange("p r n -> p (r n)")
        x_half = [t[:, :].rearrange("p (g t d) -> p g t d", g=2, d=D) for t in (hi_st, lo_st)]
        x_src = x.rearrange("b (g t p) d -> b g p t d", p=P, t=TB)
        wqk_src = wqk.rearrange("(c p) h m -> h p c m", p=P)
        wv_src = Wv.rearrange("(c p) n -> p c n", p=P)
        v_dst = v_scratch.rearrange("b (a h) p t c -> b a t p h c", a=2)
        out_dst = scratch.rearrange("b (n t p) (h k) -> b h n p t k", p=P, t=TB, k=K)
        hi_w = hi_st[:, :].bitcast(F32R)
        lo_w = lo_st[:, :].bitcast(F32R)

        def side_items(u, last):
            per_step = []
            for t in range(STEPS):
                j, kt = divmod(t, KT)
                ahead = 0 if j < NB - 2 else 1
                items = []
                if not (last and u == 1 and ahead):
                    items.append(("max", ahead, (j + 2) % NB, kt))
                if not last and j >= NB - 2 and kt in CHUNKS_AT:
                    items.append(("proj", 2, 2 * (j - NB + 2) + CHUNKS_AT.index(kt), 0))
                per_step.append(items)
            return per_step

        def walk(eng, prologue, head):
            with eng.Fori(0, B) as b:
                prologue(b)
                with eng.Fori(0, HH - 1) as i:
                    g = eng.snap(b * H + i * 2)
                    n = 0
                    for u in range(2):
                        n = head(b, i * 2, g, u, False, n)
                g = eng.snap(b * H + (H - 2))
                n = 0
                for u in range(2):
                    n = head(b, H - 2, g, u, True, n)

        block = ctx.enter_context(nc.Block())

        @block.sync
        def _(sp):
            sp.sem_inc(slot_full, 16)
            for u in range(2):
                sp.sem_inc(max_row[u], 16)
                sp.sem_inc(ctx_out[u], 16)
                sp.sem_inc(v_kept[u], 16)
            sp.dma_start(ident[:, :], ident_in).then_inc(const_in, 16)
            sp.dma_start(bias[:, :], bqk).then_inc(const_in, 16)

            def load_w(hd, g):
                sp.wait_ge(w_split, g + 1)
                sp.dma_start(w_raw[:, :, :], wqk_src[bass.ds(hd, 1)]).then_inc(w_in, 16)

            def fill(u, g):
                sp.wait_ge(staged, (g + 1) * NB + 1)
                for dst, src in ((qA[u][0:K], hi_st[0:K]), (qA[u][K:P], lo_st[0:K]),
                                 (kA[u][0:K], hi_st[K:P]), (kA[u][K:P], hi_st[K:P]),
                                 (qB[u][0:K], hi_st[0:K]), (kB[u][0:K], lo_st[K:P])):
                    sp.dma_start(dst.bitcast(F32), src).then_inc(slot_full, 16)

            def load_v(b, hd, u):
                sp.dma_start(V[u][:, :, :], v_scratch[bass.ds(b, 1), bass.ds(hd, 1)]).then_inc(v_full[u], 16)

            def max_row_in(u, blk, n):
                sp.wait_ge(negm_ready, n + 1)
                dst = qB[u][K:K + 1, blk * BLK:(blk + 1) * BLK].rearrange("o (p t) -> o p t", t=TB)
                sp.dma_start(dst.bitcast(F32), negm[:, blk % 2, :].bitcast(F32)).then_inc(max_row[blk % 2], 16)

            def prologue(b):
                g = sp.snap(b * H)
                sp.wait_ge(slot_full, g * 96 + 16)
                for k in range(NB):
                    sp.dma_start(x_half[k // 2][:, k % 2], x_src[bass.ds(b, 1), k]).then_inc(x_in, 16)
                load_w(0, g)
                sp.wait_ge(pv_done, g * STEPS + PROBS)
                sp.dma_start(wv_raw, wv_src).then_inc(wv_in, 16)
                fill(0, g)
                load_w(1, g + 1)
                sp.wait_ge(wv_ready, b + 1)
                sp.dma_start(bv_all, bv.rearrange("(o n) -> o n", o=1).to_broadcast([P, H * K])).then_inc(bv_in, 16)
                for k in range(KT * 2):
                    sp.wait_ge(v_ready, b * KT * 2 + k + 1)
                    sp.dma_start(v_dst[bass.ds(b, 1), k % 2, k // 2], v_new[:, k % 2]).then_inc(v_kept[k % 2], 16)
                for u in range(2):
                    sp.wait_ge(v_kept[u], b * KT * 16 + KT * 16 + 16)
                load_v(b, 0, 0)
                max_row_in(0, 0, g * NB)
                max_row_in(0, 1, g * NB + 1)

            def head(b, i, g, u, last, n):
                if not (last and u == 1):
                    sp.wait_ge(pv_done, (g + u) * STEPS + PROBS)
                    fill(1 - u, g + u + 1)
                    load_v(b, i + u + 1, 1 - u)
                if not last:
                    load_w(i + u + 2, g + u + 2)
                for j in range(NB):
                    ahead = 0 if j < NB - 2 else 1
                    if not (last and u == 1 and ahead):
                        max_row_in((u + ahead) % 2, (j + 2) % NB, (g + u) * NB + j + 2)
                    sp.wait_ge(ctx_ready, (g + u) * NB + j + 1)
                    sp.dma_start(out_dst[bass.ds(b, 1), bass.ds(i + u, 1), j],
                                 ctx_n[:, j % 2]).then_inc(ctx_out[j % 2], 16)
                return n

            walk(sp, prologue, head)
            for u in range(2):
                sp.wait_ge(ctx_out[u], (B * H * NB // 2 + 1) * 16)

        @block.gpsimd
        def _(pool):
            for u in range(2):
                nc.gpsimd.memset(kB[u][K:K + 1, :].bitcast(F32), 1.0).then_inc(ones_set, 1)
                pool.wait_ge(ones_set, u + 1)

            def head(b, i, g, u, last, n):
                for t in range(STEPS):
                    if lo_on_dve(t):
                        continue
                    r = t % PROBS
                    pool.wait_ge(exp_done, (g + u) * STEPS + t + 1 + RING)
                    nc.gpsimd.tensor_tensor(p_l[:, r], p_f[:, r], p_h[:, r], ALU.subtract).then_inc(lo_pool, 1)
                return n

            walk(pool, lambda b: None, head)

        @block.scalar
        def _(act):
            act.sem_inc(exp_done, RING)

            def prologue(b):
                for k in range(NB * DT):
                    g, c = divmod(k, DT)
                    act.wait_ge(pro_full, b * PRO + k + 1)
                    nc.scalar.activation(xTh[:, c, g * BLK:(g + 1) * BLK], ps_score[:, k % RING], ACT.Copy)\
                        .then_inc(xh_ready, 1)
                act.wait_ge(wv_in, b * 16 + 16)
                nc.scalar.activation(wvh_v, wv_raw, ACT.Copy).then_inc(wvh_ready, 1)
                for k in range(KT * 2):
                    act.wait_ge(pro_free, b * PRO + NB * DT + k + 1 + RING)
                    vf = p_f[:, 2 + k % 2].rearrange("p (h k) -> p h k", k=K)
                    act.wait_ge(v_kept[k % 2], b * KT * 16 + k // 2 * 16 + 16)
                    nc.scalar.activation(v_new[:, k % 2, :, 0:K], vf, ACT.Copy).then_inc(vh_ready, 1)
                    act.wait_ge(vd_ready, b * KT * 2 + k + 1)
                    nc.scalar.activation(v_new[:, k % 2, :, K + 1:VW], vf, ACT.Copy, scale=LO_SCALE).then_inc(v_ready, 1)

            def head(b, i, g, u, last, n):
                for t in range(STEPS):
                    r, bank = t % PROBS, t % RING
                    act.wait_ge(s_full, (g + u) * STEPS + t + 1)
                    act.wait_ge(pv_done, (g + u) * STEPS + t + 1)
                    nc.scalar.activation(p_f[:, r], ps_score[:, bank], ACT.Exp, scale=K ** -0.5)
                    nc.scalar.activation(p_h[:, r], ps_score[:, bank], ACT.Exp, scale=K ** -0.5).then_inc(exp_done, 1)
                return n

            walk(act, prologue, head)

        @block.vector
        def _(dve):
            dve.sem_inc(pro_free, RING)
            dve.sem_inc(max_read, 2)
            dve.sem_inc(ctx_free, 1)
            dve.sem_inc(w_split, 1)
            dve.sem_inc(staged, 1)
            nc.vector.memset(v_new[:, :, :, K:K + 1], 1.0)
            dve.wait_ge(const_in, 32)

            def split_w(hd, g):
                dve.wait_ge(staged, g * NB + 1)
                nc.vector.tensor_copy(b_cur[:, :], bias[:, bass.ds(hd, 1)])
                dve.wait_ge(w_in, g * 16 + 16)
                nc.vector.tensor_copy(w_h[:, :, :], w_raw[:, :, :]).then_inc(wh_ready, 1)
                dve.wait_ge(wh_ready, g + 1)
                nc.vector.tensor_tensor(w_l[:, :, :], w_raw[:, :, :], w_h[:, :, :].bitcast(F32),
                                        ALU.subtract).then_inc(w_split, 1)

            def stage(g, chunk, n, bank):
                cols = slice(chunk * BLK, (chunk + 1) * BLK)
                if chunk == 0:
                    dve.wait_ge(w_split, g + 2)
                    dve.wait_ge(slot_full, g * 96 + 16)
                dve.wait_ge(aux_full, n + 1)
                b_col = b_cur[:, 0:1]
                nc.vector.tensor_scalar(hi_w[:, cols], ps_aux[:, bank], b_col, None, ALU.add).then_inc(hi_ready, 1)
                dve.wait_ge(hi_ready, g * NB + chunk + 1)
                nc.vector.scalar_tensor_tensor(out=lo_w[:, cols], in0=ps_aux[:, bank], scalar=b_col,
                                               in1=hi_st[:, cols], op0=ALU.add, op1=ALU.subtract)\
                    .then_inc(staged, 1)

            def maximum(hd, blk, kt, n, m, bank):
                tt, ch = divmod(kt, NB)
                dve.wait_ge(aux_full, n + 1)
                nc.vector.reduce_max(mx[:, blk % 2, tt, ch:ch + 1], ps_aux[:, bank], AX_X).then_inc(max_read, 1)
                if kt == KT - 1:
                    dve.wait_ge(max_read, m + 1 + 2)
                    nc.vector.reduce_max(mrow[:, blk % 2], mx[:, blk % 2], AX_X).then_inc(max_step, 1)
                    dve.wait_ge(max_step, hd * NB + blk + 1)
                    dve.wait_ge(max_row[blk % 2], (hd * (NB // 2) + blk // 2) * 16 + 16)
                    nc.vector.tensor_scalar(negm[:, blk % 2], mrow[:, blk % 2], -1.0, P_SHIFT * K ** 0.5,
                                            ALU.mult, ALU.add).then_inc(negm_ready, 1)

            def low(hd, t):
                if lo_on_dve(t):
                    r = t % PROBS
                    dve.wait_ge(exp_done, hd * STEPS + t + 1 + RING)
                    nc.vector.tensor_tensor(p_l[:, r], p_f[:, r], p_h[:, r], ALU.subtract).then_inc(lo_dve, 1)

            def evacuate(j, hd):
                nb = hd * NB + j
                dve.wait_ge(pv_done, (nb + 1) * KT + PROBS)
                acc = ps_ctx[:, :, 0:2 * VW].rearrange("p a (t c) -> p a t c", c=VW)
                four = lambda ap: ap.rearrange("p (a t) k -> p a t k", a=2)
                nc.vector.tensor_scalar(four(b_sum[:, :, :]), acc[:, :, :, K + 1:VW], 1.0 / LO_SCALE, None,
                                        ALU.mult).then_inc(ev_step, 1)
                nc.vector.reciprocal(rden[:, :].rearrange("p (a t) -> p a t", a=2), acc[:, :, :, K])\
                    .then_inc(ev_step, 1)
                dve.wait_ge(ev_step, nb * 2 + 2)
                nc.vector.tensor_tensor(four(ctx_u[:, :, :]), acc[:, :, :, 0:K], four(b_sum[:, :, :]),
                                        ALU.add).then_inc(ctx_free, 1)
                dve.wait_ge(ctx_free, nb + 2)
                dve.wait_ge(ctx_out[j % 2], (hd * (NB // 2) + j // 2) * 16 + 16)
                nc.vector.tensor_tensor(ctx_n[:, j % 2], ctx_u[:, :, :],
                                        rden[:, :].unsqueeze(2).to_broadcast([P, TB, K]), ALU.mult)\
                    .then_inc(ctx_ready, 1)

            def prologue(b):
                g0 = dve.snap(b * H)
                a0 = dve.snap(g0 * AUX)
                dve.wait_ge(x_in, b * 64 + 64)
                for k in range(NB):
                    xg = x_half[k // 2][:, k % 2]
                    norm(nc, dve, xg, xg, EPS_LN, small, ln_step, (b * NB + k) * NORM)
                for k in range(NB * DT):
                    gr, c = divmod(k, DT)
                    dve.wait_ge(xh_ready, b * NB * DT + k + 1)
                    cols = slice(gr * BLK, (gr + 1) * BLK)
                    nc.vector.tensor_tensor(xTl[:, c, cols], ps_score[:, k % RING], xTh[:, c, cols].bitcast(F32),
                                            ALU.subtract).then_inc(pro_free, 1)
                split_w(0, g0)
                for c in range(NB):
                    stage(g0, c, a0 + c, c % 2)
                dve.wait_ge(wvh_ready, b + 1)
                nc.vector.tensor_tensor(wvl_v, wv_raw, wvh_v.bitcast(F32), ALU.subtract).then_inc(wv_ready, 1)
                split_w(1, g0 + 1)
                dve.wait_ge(bv_in, b * 16 + 16)
                for k in range(KT * 2):
                    half = k % 2
                    dve.wait_ge(pro_full, b * PRO + NB * DT + k + 1)
                    if k >= 2:
                        dve.wait_ge(v_ready, b * KT * 2 + k - 1)
                    vf = p_f[:, 2 + k % 2]
                    nc.vector.tensor_tensor(vf, ps_score[:, k % RING], bv_all[:, half * BLK:(half + 1) * BLK],
                                            ALU.add).then_inc(pro_free, 1)
                    dve.wait_ge(vh_ready, b * KT * 2 + k + 1)
                    vf3 = vf.rearrange("p (h k) -> p h k", k=K)
                    nc.vector.tensor_tensor(vf3, vf3, v_new[:, k % 2, :, 0:K],
                                            ALU.subtract).then_inc(vd_ready, 1)
                for c in range(NB):
                    stage(g0 + 1, c, a0 + NB + c, c % 2)
                for blk in range(2):
                    for kt in range(KT):
                        maximum(g0, blk, kt, a0 + 2 * NB + blk * KT + kt, g0 * STEPS + blk * KT + kt, kt % 2)
                for t in range(LO_AHEAD):
                    low(g0, t)

            def head(b, i, g, u, last, n):
                items = side_items(u, last)
                for t in range(STEPS):
                    j, kt = divmod(t, KT)
                    if t + LO_AHEAD < STEPS:
                        low(g + u, t + LO_AHEAD)
                    elif not (last and u == 1):
                        low(g + u + 1, t + LO_AHEAD - STEPS)
                    if kt == 0 and j > 0:
                        evacuate(j - 1, g + u)
                    if t == 0 and u == 1:
                        evacuate(NB - 1, g)
                    for kind, ahead, a, k in items[t]:
                        if kind == "max":
                            maximum(g + u + ahead, a, k, g * AUX + PRO_AUX + n,
                                    (g + u) * STEPS + 2 * KT + t, n % 2)
                        else:
                            stage(g + u + 2, a, g * AUX + PRO_AUX + n, n % 2)
                        n += 1
                    if t == KT + 4 and not last:
                        split_w(i + u + 2, g + u + 2)
                if u == 1:
                    evacuate(NB - 1, g + 1)
                return n

            walk(dve, prologue, head)

        @block.tensor
        def _(pe):
            pe.sem_inc(pv_done, PROBS)
            pe.wait_ge(const_in, 32)
            pe.wait_ge(ones_set, 2)

            used = []

            def after_maxima(m):
                used[:] = [(max_read, m + 1), (max_read, m + 2)]

            def project(g, chunk, bank):
                if chunk == 0:
                    pe.wait_ge(w_split, g + 2)
                pe.wait_ge(*used.pop(0))
                used.append((staged, g * NB + chunk + 2))
                cols = slice(chunk * BLK, (chunk + 1) * BLK)
                parts = [(w, t, c) for c in range(DT) for w, t in ((w_h, xTh), (w_l, xTh), (w_h, xTl))]
                for m, (w, t, c) in enumerate(parts):
                    mm = nc.tensor.matmul(ps_aux[:, bank], w[:, c], t[:, c, cols],
                                          start=(m == 0), stop=(m == len(parts) - 1))
                mm.then_inc(aux_full, 1)

            def max_tile(u, g, blk, kt, m, bank):
                tt, ch = divmod(kt, NB)
                if blk % 2 == 0 and kt == 0:
                    pe.wait_ge(slot_full, g * 96 + 96 + 16)
                pe.wait_ge(*used.pop(0))
                used.append((max_read, m + 3))
                q = qA[u][:, blk * BLK:(blk + 1) * BLK].rearrange("k (p t) -> k t p", t=TB)[:, tt]
                nc.tensor.matmul(ps_aux[:, bank], q, kA[u][:, ch * BLK:(ch + 1) * BLK],
                                 start=True, stop=True).then_inc(aux_full, 1)

            def score(u, g, t):
                j, kt = divmod(t, KT)
                if kt == 0:
                    pe.wait_ge(max_row[j % 2], (g * (NB // 2) + j // 2) * 16 + 32)
                pe.wait_ge(exp_done, g * STEPS + t + 1)
                keys, cols = slice(kt * P, (kt + 1) * P), slice(j * BLK, (j + 1) * BLK)
                nc.tensor.matmul(ps_score[:, t % RING], kA[u][:, keys], qA[u][:, cols], start=True, stop=False)
                nc.tensor.matmul(ps_score[:, t % RING], kB[u][:, keys], qB[u][:, cols],
                                 start=False, stop=True).then_inc(s_full, 1)

            def weigh(u, g, t):
                j, kt = divmod(t, KT)
                r = t % PROBS
                if kt == 0:
                    pe.wait_ge(ctx_free, (g + u) * NB + j + 1)
                if t == 0:
                    pe.wait_ge(v_full[u], g * 8 + 16)
                nd, npl = lo_counts(t)
                if lo_on_dve(t):
                    pe.wait_ge(lo_dve, (g + u) * DVE_LO + nd)
                else:
                    pe.wait_ge(lo_pool, (g + u) * POOL_LO + npl)
                for q in range(TB):
                    acc = ps_ctx[:, q // 2, (q % 2) * VW:(q % 2 + 1) * VW]
                    vt = V[u][:, kt]
                    nc.tensor.matmul(acc, p_h[:, r, q * P:(q + 1) * P], vt,
                                     start=(kt == 0 and q % 2 == 0), stop=False, skip_group_check=True)
                    mm = nc.tensor.matmul(acc[:, 0:K + 1], p_l[:, r, q * P:(q + 1) * P], vt[:, 0:K + 1],
                                          start=False, stop=(kt == KT - 1 and q % 2 == 1),
                                          skip_group_check=True)
                mm.then_inc(pv_done, 1)

            def prologue(b):
                g0 = pe.snap(b * H)
                after_maxima(g0 * STEPS)
                pe.wait_ge(exp_done, g0 * STEPS + RING)
                for k in range(NB * DT):
                    gr, c = divmod(k, DT)
                    pe.wait_ge(ln_step, (b * NB + gr + 1) * NORM)
                    pe.wait_ge(pro_free, b * PRO + k + 1)
                    xg = x_half[gr // 2][:, gr % 2]
                    for t in range(TB):
                        mm = nc.tensor.transpose(ps_score[:, k % RING, t * P:(t + 1) * P],
                                                 xg[:, t, c * P:(c + 1) * P], ident[:, :])
                    mm.then_inc(pro_full, 1)
                pe.wait_ge(pro_free, b * PRO + NB * DT + RING)
                for c in range(NB):
                    project(g0, c, c % 2)
                pe.wait_ge(wv_ready, b + 1)
                for k in range(KT * 2):
                    tt, half = divmod(k, 2)
                    pe.wait_ge(pro_free, b * PRO + NB * DT + k + 1)
                    toks, cols = slice(tt * P, (tt + 1) * P), slice(half * BLK, (half + 1) * BLK)
                    parts = [(t, w, c) for c in range(DT)
                             for t, w in ((xTh, wvh_v), (xTh, wvl_v), (xTl, wvh_v))]
                    for m, (t, w, c) in enumerate(parts):
                        mm = nc.tensor.matmul(ps_score[:, k % RING], t[:, c, toks], w[:, c, cols],
                                              start=(m == 0), stop=(m == len(parts) - 1))
                    mm.then_inc(pro_full, 1)
                for c in range(NB):
                    project(g0 + 1, c, c % 2)
                for blk in range(2):
                    for kt in range(KT):
                        max_tile(0, g0, blk, kt, g0 * STEPS + blk * KT + kt, kt % 2)
                pe.wait_ge(pro_free, b * PRO + PRO + RING)
                for t in range(AHEAD):
                    score(0, g0, t)

            def head(b, i, g, u, last, n):
                items = side_items(u, last)
                if u == 0:
                    after_maxima(g * STEPS + 2 * KT)
                for t in range(STEPS):
                    j, kt = divmod(t, KT)
                    for kind, ahead, a, k in items[t]:
                        if kind == "max":
                            max_tile((u + ahead) % 2, g + u + ahead, a, k, (g + u) * STEPS + 2 * KT + t, n % 2)
                        else:
                            project(g + u + 2, a, n % 2)
                        n += 1
                    if t + AHEAD < STEPS:
                        score(u, g + u, t + AHEAD)
                    elif not (last and u == 1):
                        score(1 - u, g + u + 1, t + AHEAD - STEPS)
                    for k in {0: (), 1: (t - 1, t)}.get(kt, (t,)):
                        weigh(u, g, k)
                return n

            walk(pe, prologue, head)


def feed_forward(nc, x, scratch, Wo, bo, gamma, beta, wgT, wuT, wdT, ident_in, out):
    B, S, D = x.shape
    HK = Wo.shape[0]
    F = wgT.shape[1]
    DT, CT, FT = D // P, HK // P, F // P
    TB = BLK // P
    G = B * S // BLK
    NA = CT + 2
    ND = DT + 2
    NS = 4 * NORM + 2
    assert DT == 2 and G % 2 == 0

    with ExitStack() as ctx:
        sb = lambda n, s, d: ctx.enter_context(nc.sbuf_tensor(n, s, d))
        sem = lambda n: ctx.enter_context(nc.semaphore(n))
        bank = lambda n, k: ctx.enter_context(nc.psum_tensor(n, [P, k, BLK], F32))
        ps_a = bank("ps_a", 2)
        ps_y = bank("ps_y", 2)
        ps_d = bank("ps_d", 2)
        ps_gu = bank("ps_gu", 2)

        id2 = sb("id2", [P, P], F32)
        bo_c = sb("bo_c", [P, DT], F32)
        gam = sb("gam", [P, D], F32)
        bet = sb("bet", [P, D], F32)
        raw = sb("raw", [P, DT * F], F32)
        raw_i = sb("raw_i", [P, DT * F], I32)
        wo = [sb(f"wo{m}", [P, CT, D], F32R) for m in "hl"]
        wg = [sb(f"wg{m}", [P, DT, F], F32R) for m in "hl"]
        wu = [sb(f"wu{m}", [P, DT, F], F32R) for m in "hl"]
        wd = [sb(f"wd{m}", [P, FT, D], F32R) for m in "hl"]
        c_in = sb("c_in", [P, TB, HK], F32)
        x_t = sb("x_t", [P, TB, D], F32)
        cT = [sb(f"cT{m}", [P, CT, BLK], F32R) for m in "hl"]
        yT = sb("yT", [P, DT, BLK], F32)
        xn = sb("xn", [P, TB, D], F32)
        z = sb("z", [P, TB, D], F32)
        x1 = [sb(f"x1_{u}", [P, TB, D], F32) for u in range(2)]
        xn2 = sb("xn2", [P, TB, D], F32)
        oT = sb("oT", [P, DT, BLK], F32)
        nT = [sb(f"nT{m}", [P, DT, BLK], F32R) for m in "hl"]
        sg = sb("sg", [P, BLK], F32)
        hf = sb("hf", [P, 2, BLK], F32)
        hT = [sb(f"hT{m}", [P, FT, BLK], F32R) for m in "hl"]
        st2 = sb("st2", [P, TB, 6], F32)
        mv2 = sb("mv2", [P, TB, 2], F32)
        small = (st2, mv2, *(sb(f"norm2_{k}", [P, TB], F32) for k in range(3)))

        s_const = sem("s_const")
        raw_in = sem("raw_in")
        raw_f = sem("raw_f")
        raw_hi = sem("raw_hi")
        raw_done = sem("raw_done")
        c_loaded = sem("c_loaded")
        x_loaded = sem("x_loaded")
        a_full = sem("a_full")
        a_free = sem("a_free")
        c_hi = sem("c_hi")
        y_full = sem("y_full")
        y_read = sem("y_read")
        norm_step = sem("norm_step")
        x_used = sem("x_used")
        d_full = sem("d_full")
        d_free = sem("d_free")
        n_hi = sem("n_hi")
        g_full = sem("g_full")
        silu_done = sem("silu_done")
        u_full = sem("u_full")
        h_ready = sem("h_ready")
        h_hi = sem("h_hi")
        h_lo = sem("h_lo")
        o_full = sem("o_full")
        o_read = sem("o_read")
        end_step = sem("end_step")
        res_ready = sem("res_ready")
        stored = [sem(f"stored{u}") for u in range(2)]

        xv = x.rearrange("b (g t p) d -> (b g) p t d", p=P, t=TB)
        ov = out.rearrange("b (g t p) d -> (b g) p t d", p=P, t=TB)
        cv = scratch.rearrange("b (g t p) n -> (b g) p t n", p=P, t=TB)
        weights = [(Wo.rearrange("(c p) n -> p c n", p=P), wo, False),
                   (wgT.rearrange("(c p) n -> p c n", p=P), wg, True),
                   (wuT.rearrange("(c p) n -> p c n", p=P), wu, True),
                   (wdT.rearrange("(c p) n -> p c n", p=P), wd, True)]

        def pieces():
            for src, dst, ints in weights:
                c, n = src.shape[1], src.shape[2]
                k = max(1, DT * F // n)
                for a in range(0, c, k):
                    e = min(c, a + k)
                    yield src[:, a:e], [d[:, a:e] for d in dst], ints, (e - a, n)

        def walk(eng, before, after):
            before(0, 0)
            with eng.Fori(0, G // 2 - 1) as i:
                g = eng.snap(i * 2)
                before(g + 1, 1)
                after(g, 0)
                before(g + 2, 0)
                after(g + 1, 1)
            before(G - 1, 1)
            after(G - 2, 0)
            after(G - 1, 1)

        block = ctx.enter_context(nc.Block())

        @block.sync
        def _(sp):
            row = lambda v: v.rearrange("(o n) -> o n", o=1).to_broadcast([P, D])
            for u in range(2):
                sp.sem_inc(stored[u], 16)
            sp.dma_start(id2[:, :], ident_in).then_inc(s_const, 16)
            sp.dma_start(bo_c[:, :], bo).then_inc(s_const, 16)
            sp.dma_start(gam[:, :], row(gamma)).then_inc(s_const, 16)
            sp.dma_start(bet[:, :], row(beta)).then_inc(s_const, 16)
            for n, (src, dst, ints, (c, w)) in enumerate(pieces()):
                if n:
                    sp.wait_ge(raw_done, n)
                to = raw_i if ints else raw
                sp.dma_start(to[:, 0:c * w].rearrange("p (c n) -> p c n", c=c), src).then_inc(raw_in, 16)

            def before(g, u):
                sp.wait_ge(a_free, g * NA + 2)
                sp.dma_start(c_in[:, :, :], cv[bass.ds(g, 1)]).then_inc(c_loaded, 16)
                sp.wait_ge(x_used, g + 1)
                sp.dma_start(x_t[:, :, :], xv[bass.ds(g, 1)]).then_inc(x_loaded, 16)

            def after(g, u):
                sp.wait_ge(res_ready, g + 1)
                sp.dma_start(ov[bass.ds(g, 1)], x1[u][:, :, :]).then_inc(stored[u], 16)

            walk(sp, before, after)
            for u in range(2):
                sp.wait_ge(stored[u], 16 * (G // 2 + 1))

        @block.scalar
        def _(act):
            act.sem_inc(o_read, 2 * DT)
            act.sem_inc(silu_done, 1)
            act.wait_ge(s_const, 64)

            def before(g, u):
                for k in range(CT):
                    act.wait_ge(a_full, g * NA + k + 1)
                    nc.scalar.activation(cT[0][:, k], ps_a[:, k % 2], ACT.Copy).then_inc(c_hi, 1)
                for c in range(DT):
                    act.wait_ge(y_full, g * DT + c + 1)
                    nc.scalar.activation(yT[:, c], ps_y[:, c], ACT.Identity, bias=bo_c[:, c:c + 1])\
                        .then_inc(y_read, 1)

            def after(g, u):
                for c in range(DT):
                    act.wait_ge(d_full, g * ND + c + 1 + ND)
                    nc.scalar.activation(nT[0][:, c], ps_d[:, c], ACT.Copy).then_inc(n_hi, 1)
                act.wait_ge(o_full, g * DT + DT)
                for f in range(FT):
                    act.wait_ge(g_full, g * FT + f + 1)
                    act.wait_ge(h_ready, g * FT + f + 1)
                    nc.scalar.activation(sg[:, :], ps_gu[:, 0], ACT.Silu).then_inc(silu_done, 1)
                    act.wait_ge(h_ready, g * FT + f + 2)
                    nc.scalar.activation(hT[0][:, f], hf[:, f % 2], ACT.Copy).then_inc(h_hi, 1)
                for c in range(DT):
                    act.wait_ge(o_full, g * DT + c + 1 + DT)
                    nc.scalar.activation(oT[:, c], ps_y[:, c], ACT.Copy).then_inc(o_read, 1)

            walk(act, before, after)

        @block.gpsimd
        def _(pool):
            pool.sem_inc(h_lo, 2)

            def after(g, u):
                for f in range(FT):
                    pool.wait_ge(h_hi, g * FT + f + 1)
                    nc.gpsimd.tensor_tensor(hT[1][:, f], hf[:, f % 2], hT[0][:, f].bitcast(F32),
                                            ALU.subtract).then_inc(h_lo, 1)

            walk(pool, lambda g, u: None, after)

        @block.vector
        def _(dve):
            dve.sem_inc(a_free, 2)
            dve.sem_inc(d_free, 2)
            dve.sem_inc(h_ready, 1)
            dve.sem_inc(x_used, 1)
            dve.wait_ge(s_const, 64)
            quantised = 0
            for n, (src, dst, ints, (c, w)) in enumerate(pieces()):
                dve.wait_ge(raw_in, 16 * (n + 1))
                flat = raw[:, 0:c * w].rearrange("p (c n) -> p c n", c=c)
                if ints:
                    if n:
                        dve.wait_ge(raw_done, n)
                    ri = raw_i[:, 0:c * w].rearrange("p (c n) -> p c n", c=c)
                    nc.vector.tensor_scalar(flat, ri, 1.0 / 127.0, None, ALU.mult).then_inc(raw_f, 1)
                    quantised += 1
                    dve.wait_ge(raw_f, quantised)
                nc.vector.tensor_copy(dst[0], flat).then_inc(raw_hi, 1)
                dve.wait_ge(raw_hi, n + 1)
                nc.vector.tensor_tensor(dst[1], flat, dst[0].bitcast(F32), ALU.subtract).then_inc(raw_done, 1)

            def before(g, u):
                s0 = g * NS
                for k in range(CT):
                    dve.wait_ge(c_hi, g * CT + k + 1)
                    nc.vector.tensor_tensor(cT[1][:, k], ps_a[:, k % 2], cT[0][:, k].bitcast(F32),
                                            ALU.subtract).then_inc(a_free, 1)
                dve.wait_ge(x_loaded, g * 16 + 16)
                norm(nc, dve, xn, x_t, EPS_LN, small, norm_step, s0)
                for c in range(2):
                    dve.wait_ge(a_full, g * NA + CT + c + 1)
                    half = slice(2 * c, 2 * c + 2)
                    nc.vector.tensor_tensor(z[:, half], ps_a[:, c].rearrange("p (t d) -> p t d", d=D), xn[:, half],
                                            ALU.add).then_inc(a_free, 1)
                dve.wait_ge(a_free, g * NA + NA + 2)
                norm(nc, dve, xn, z, EPS_ATTN, small, norm_step, s0 + NORM)
                wide = lambda v: v[:, :].unsqueeze(1).to_broadcast([P, TB, D])
                nc.vector.tensor_tensor(xn[:, :, :], xn[:, :, :], wide(gam), ALU.mult).then_inc(norm_step, 1)
                dve.wait_ge(norm_step, s0 + 2 * NORM + 1)
                nc.vector.tensor_tensor(xn[:, :, :], xn[:, :, :], wide(bet), ALU.add).then_inc(norm_step, 1)
                dve.wait_ge(norm_step, s0 + 2 * NORM + 2)
                norm(nc, dve, z, xn, EPS_LN, small, norm_step, s0 + 2 * NORM + 2)
                dve.wait_ge(stored[u], (g - u) * 8 + 16)
                nc.vector.tensor_tensor(x1[u][:, :, :], x_t[:, :, :], z[:, :, :], ALU.add).then_inc(x_used, 1)
                dve.wait_ge(x_used, g + 2)
                dve.wait_ge(d_full, g * ND + DT)
                norm(nc, dve, xn2, x1[u], EPS_LN, small, norm_step, s0 + 3 * NORM + 2)

            def after(g, u):
                for c in range(DT):
                    dve.wait_ge(n_hi, g * DT + c + 1)
                    nc.vector.tensor_tensor(nT[1][:, c], ps_d[:, c], nT[0][:, c].bitcast(F32),
                                            ALU.subtract).then_inc(d_free, 1)
                for f in range(FT):
                    dve.wait_ge(u_full, g * FT + f + 1)
                    dve.wait_ge(silu_done, g * FT + f + 2)
                    dve.wait_ge(h_lo, g * FT + f + 1)
                    nc.vector.tensor_tensor(hf[:, f % 2], ps_gu[:, 1], sg[:, :], ALU.mult).then_inc(h_ready, 1)
                for c in range(2):
                    dve.wait_ge(d_full, g * ND + DT + c + 1 + ND)
                    nc.vector.tensor_copy(z[:, 2 * c:2 * c + 2], ps_d[:, c].rearrange("p (t d) -> p t d", d=D))\
                        .then_inc(d_free, 1)
                dve.wait_ge(d_free, g * ND + ND + 2)
                norm(nc, dve, z, z, EPS_LN, small, end_step, g * NORM)
                nc.vector.tensor_tensor(x1[u][:, :, :], x1[u][:, :, :], z[:, :, :], ALU.add).then_inc(res_ready, 1)

            walk(dve, before, after)

        @block.tensor
        def _(pe):
            pe.sem_inc(d_full, ND)
            pe.sem_inc(o_full, DT)
            pe.wait_ge(s_const, 64)
            pe.wait_ge(raw_done, len(list(pieces())))

            def product(dst, terms):
                passes = [(w[m], t[k]) for w, t in terms for m, k in ((0, 0), (1, 0), (0, 1))]
                for n, (w, t) in enumerate(passes):
                    mm = nc.tensor.matmul(dst, w, t, start=(n == 0), stop=(n == len(passes) - 1))
                return mm

            def turn_back(dst, src, c):
                for t in range(2):
                    for w in range(DT):
                        mm = nc.tensor.transpose(dst[:, (t * DT + w) * P:(t * DT + w + 1) * P],
                                                 src[:, w, (2 * c + t) * P:(2 * c + t + 1) * P], id2[:, :])
                return mm

            def before(g, u):
                pe.wait_ge(c_loaded, g * 16 + 16)
                for k in range(CT):
                    pe.wait_ge(a_free, g * NA + k + 1)
                    for t in range(TB):
                        mm = nc.tensor.transpose(ps_a[:, k % 2, t * P:(t + 1) * P],
                                                 c_in[:, t, k * P:(k + 1) * P], id2[:, :])
                    mm.then_inc(a_full, 1)
                pe.wait_ge(a_free, g * NA + CT + 2)
                pe.wait_ge(o_read, (g + 1) * DT)
                for c in range(DT):
                    product(ps_y[:, c], [([w[:, k, c * P:(c + 1) * P] for w in wo], [t[:, k] for t in cT])
                                         for k in range(CT)]).then_inc(y_full, 1)
                pe.wait_ge(y_read, g * DT + DT)
                for c in range(2):
                    pe.wait_ge(a_free, g * NA + CT + c + 1)
                    turn_back(ps_a[:, c], yT, c).then_inc(a_full, 1)

            def after(g, u):
                pe.wait_ge(norm_step, g * NS + NS)
                for c in range(DT):
                    pe.wait_ge(d_free, g * ND + c + 1)
                    for t in range(TB):
                        mm = nc.tensor.transpose(ps_d[:, c, t * P:(t + 1) * P], xn2[:, t, c * P:(c + 1) * P],
                                                 id2[:, :])
                    mm.then_inc(d_full, 1)
                pe.wait_ge(d_free, g * ND + DT + 2)
                for f in range(FT):
                    fs = slice(f * P, (f + 1) * P)
                    for m, (w, full, free) in enumerate(((wg, g_full, silu_done), (wu, u_full, h_ready))):
                        pe.wait_ge(free, g * FT + f + 1)
                        product(ps_gu[:, m], [([v[:, c, fs] for v in w], [t[:, c] for t in nT])
                                              for c in range(DT)]).then_inc(full, 1)
                pe.wait_ge(h_lo, g * FT + FT + 2)
                pe.wait_ge(y_read, G * DT if isinstance(g, int) else (g + 2) * DT)
                for c in range(DT):
                    product(ps_y[:, c], [([w[:, f, c * P:(c + 1) * P] for w in wd], [t[:, f] for t in hT])
                                         for f in range(FT)]).then_inc(o_full, 1)
                pe.wait_ge(o_read, (g + 3) * DT)
                for c in range(2):
                    pe.wait_ge(d_free, g * ND + DT + c + 1)
                    turn_back(ps_d[:, c], oT, c).then_inc(d_full, 1)

            walk(pe, before, after)


def program(nc, x, wqk, bqk, Wv, bv, Wo, bo, gamma, beta, wgT, wuT, wdT, ident, out):
    B, S, _ = x.shape
    scratch = nc.dram_tensor("heads", (B, S, Wo.shape[0]), F32, kind="Internal").ap()
    v_scratch = nc.dram_tensor("v_heads", (B, wqk.shape[1], P, S // P, wqk.shape[2] + 1), F16, kind="Internal").ap()
    nc.disable_value_cache = True
    attention(nc, x, wqk, bqk, Wv, bv, ident, v_scratch, scratch)
    feed_forward(nc, x, scratch, Wo, bo, gamma, beta, wgT, wuT, wdT, ident, out)


def kernel(L0_attn_x, L0_attn_Wq, L0_attn_bq, L0_attn_Wk, L0_attn_bk, L0_attn_Wv, L0_attn_bv, L0_attn_Wo,
           L0_attn_bo, L0_attn_gamma, L0_attn_beta, L0_ffn_w_gate, L0_ffn_w_up, L0_ffn_w_down):
    import numpy as np
    import concourse.bacc as bacc
    from concourse.bass_utils import run_bass_kernel_spmd

    a = lambda v: np.ascontiguousarray(v)
    D, H, K = L0_attn_Wq.shape
    arrays = {
        "x": a(L0_attn_x),
        "wqk": a(np.concatenate([L0_attn_Wq, L0_attn_Wk], axis=2)),
        "bqk": a(np.concatenate([L0_attn_bq, L0_attn_bk], axis=1).T),
        "Wv": a(np.reshape(L0_attn_Wv, (D, H * K))),
        "bv": a(np.reshape(L0_attn_bv, (H * K,))),
        "Wo": a(np.reshape(L0_attn_Wo, (H * K, D))),
        "bo": a(np.reshape(L0_attn_bo, (D // P, P)).T),
        "gamma": a(L0_attn_gamma),
        "beta": a(L0_attn_beta),
        "wgT": a(np.transpose(L0_ffn_w_gate)),
        "wuT": a(np.transpose(L0_ffn_w_up)),
        "wdT": a(np.transpose(L0_ffn_w_down)),
        "ident": np.eye(P, dtype=np.float32),
    }
    nc = bacc.Bacc("TRN2", target_bir_lowering=False, num_devices=1)
    args = [nc.dram_tensor(f"in_{n}", v.shape, mybir.dt.from_np(v.dtype), kind="ExternalInput").ap()
            for n, v in arrays.items()]
    out = nc.dram_tensor("out", arrays["x"].shape, F32, kind="ExternalOutput").ap()
    program(nc, *args, out)
    r = run_bass_kernel_spmd(nc, [{f"in_{n}": v for n, v in arrays.items()}], core_ids=[0])
    return r.results[0]["out"]
```

```python
from contextlib import ExitStack

import concourse.bass as bass
from concourse import mybir

P = 128
ALU = mybir.AluOpType
ACT = mybir.ActivationFunctionType
F32 = mybir.dt.float32
F32R = mybir.dt.float32r
F16 = mybir.dt.float16
I32 = mybir.dt.int32
AX_X = mybir.AxisListType.X

EPS_LN = 1e-5
EPS_ATTN = 1e-3
BLK = 512
RING = 4
PROBS = 8
AHEAD = 6
CHUNK_LAG = 4
LO_AHEAD = 3
P_SHIFT = 5.545177444479562
LO_SCALE = 2048.0
SUMS_AT = 4
CHUNKS_AT = (3, 9)


def lo_on_dve(t):
    return t % 8 in (1, 3, 5)


def lo_counts(t):
    dve = sum(lo_on_dve(k) for k in range(t + 1))
    return dve, t + 1 - dve


ROOT = 14
NORM = ROOT + 1
RSQRT_SEED = float(0x5F3759DF)


def root(nc, dve, src, eps, small, step, value):
    stats, mv, v, y, w = small
    tiles = src.shape[1]
    n = [0]

    def then(ins):
        n[0] += 1
        ins.then_inc(step, 1)
        dve.wait_ge(step, value + n[0])

    for t in range(tiles):
        ins = nc.vector.bn_stats(stats[:, t], src[:, t])
    then(ins)
    nc.vector.memset(v[:, :], 0.0)
    for t in range(tiles):
        ins = nc.vector.bn_aggr(mv[:, t], stats[:, t])
    then(ins)
    then(nc.vector.tensor_scalar(v[:, :], mv[:, :, 1], eps, None, ALU.add))
    then(nc.vector.tensor_scalar(w[:, :].bitcast(I32), v[:, :].bitcast(I32), 1, None, ALU.logical_shift_right))
    then(nc.vector.tensor_scalar(y[:, :].bitcast(I32), w[:, :].bitcast(I32), -1.0, RSQRT_SEED, ALU.mult, ALU.add))
    for _ in range(3):
        then(nc.vector.tensor_tensor(w[:, :], y[:, :], y[:, :], ALU.mult))
        then(nc.vector.scalar_tensor_tensor(out=w[:, :], in0=w[:, :], scalar=-0.5, in1=v[:, :],
                                            op0=ALU.mult, op1=ALU.mult))
        then(nc.vector.scalar_tensor_tensor(out=y[:, :], in0=w[:, :], scalar=1.5, in1=y[:, :],
                                            op0=ALU.add, op1=ALU.mult))
    assert n[0] == ROOT


def norm(nc, dve, dst, src, eps, small, step, value):
    root(nc, dve, src, eps, small, step, value)
    _, mv, _, y, _ = small
    for t in range(dst.shape[1]):
        ins = nc.vector.tensor_scalar(dst[:, t], src[:, t], mv[:, t, 0:1], y[:, t:t + 1], ALU.subtract, ALU.mult)
    ins.then_inc(step, 1)
    dve.wait_ge(step, value + NORM)


def attention(nc, x, wqk, bqk, Wv, bv, ident_in, v_scratch, scratch, x_mean, x_root):
    B, S, D = x.shape
    H = wqk.shape[1]
    K = wqk.shape[2] // 2
    DT = D // P
    KT = S // P
    NB = S // BLK
    TB = BLK // P
    STEPS = NB * KT
    AUX = NB + STEPS
    PRO_AUX = 2 * NB + 2 * KT
    PRO = NB * DT + KT * 2
    VW = 2 * K + 1
    DVE_LO, POOL_LO = lo_counts(STEPS - 1)
    HH = H // 2

    with ExitStack() as ctx:
        sb = lambda n, s, d: ctx.enter_context(nc.sbuf_tensor(n, s, d))
        sem = lambda n: ctx.enter_context(nc.semaphore(n))
        ps_score = ctx.enter_context(nc.psum_tensor("ps_score", [P, RING, BLK], F32))
        ps_aux = ctx.enter_context(nc.psum_tensor("ps_aux", [P, 2, BLK], F32))
        ps_ctx = ctx.enter_context(nc.psum_tensor("ps_ctx", [P, 2, BLK], F32))

        qA = [sb(f"q_hilo{u}", [P, S], F32R) for u in range(2)]
        kA = [sb(f"k_hihi{u}", [P, S], F32R) for u in range(2)]
        qB = [sb(f"q_hi_max{u}", [K + 1, S], F32R) for u in range(2)]
        kB = [sb(f"k_lo_one{u}", [K + 1, S], F32R) for u in range(2)]
        hi_st = sb("hi_st", [P, S], F32)
        qk_new = sb("qk_new", [P, BLK], F32)
        lo_st = sb("lo_st", [P, S], F32)
        xTh = sb("xTh", [P, DT, S], F32R)
        xTl = sb("xTl", [P, DT, S], F32R)
        v_new = sb("v_new", [P, 2, HH, VW], F16)
        V = [sb(f"v_hi_one_lo{u}", [P, KT, VW], F16) for u in range(2)]
        p_f = sb("p_f", [P, PROBS, BLK], F32)
        p_h = sb("p_h", [P, PROBS, BLK], F16)
        p_l = sb("p_l", [P, PROBS, BLK], F16)
        w_raw = sb("w_raw", [P, DT, P], F32)
        w_h = sb("w_h", [P, DT, P], F32R)
        w_l = sb("w_l", [P, DT, P], F32R)
        bias = sb("bias", [P, H], F32)
        b_cur = sb("b_cur", [P, 1], F32)
        ident = sb("ident", [P, P], F32)
        mx = sb("mx", [P, 2, TB, NB], F32)
        mrow = sb("mrow", [P, 2, TB], F32)
        negm = sb("negm", [P, 2, TB], F32R)
        sums = sb("sums", [P, 2, 2 * VW], F32)
        rden = sb("rden", [P, TB], F32)
        ctx_u = sb("ctx_u", [P, TB, K], F32)
        ctx_n = sb("ctx_n", [P, 2, TB, K], F32)
        stats = sb("stats", [P, TB, 6], F32)
        mv = sb("mv", [P, TB, 2], F32)
        small = (stats, mv, *(sb(f"norm{k}", [P, TB], F32) for k in range(3)))

        const_in = sem("const_in")
        ones_set = sem("ones_set")
        x_in = sem("x_in")
        ln_step = sem("ln_step")
        pro_full = sem("pro_full")
        pro_free = sem("pro_free")
        xh_ready = sem("xh_ready")
        wv_in = sem("wv_in")
        wvh_ready = sem("wvh_ready")
        wv_ready = sem("wv_ready")
        bv_in = sem("bv_in")
        vh_ready = sem("vh_ready")
        vd_ready = sem("vd_ready")
        v_ready = sem("v_ready")
        v_kept = [sem(f"v_kept{u}") for u in range(2)]
        v_full = [sem(f"v_full{u}") for u in range(2)]
        w_in = sem("w_in")
        wh_ready = sem("wh_ready")
        w_split = sem("w_split")
        aux_full = sem("aux_full")
        max_read = sem("max_read")
        qk_ready = sem("qk_ready")
        hi_ready = sem("hi_ready")
        staged = sem("staged")
        slot_full = sem("slot_full")
        max_step = sem("max_step")
        negm_ready = sem("negm_ready")
        max_row = [sem(f"max_row{u}") for u in range(2)]
        s_full = sem("s_full")
        exp_done = sem("exp_done")
        lo_dve = sem("lo_dve")
        lo_pool = sem("lo_pool")
        pv_done = sem("pv_done")
        ev_step = sem("ev_step")
        ctx_free = sem("ctx_free")
        ctx_ready = sem("ctx_ready")
        ctx_out = [sem(f"ctx_out{u}") for u in range(2)]

        wvh_v = qA[1][:, :].rearrange("p (c n) -> p c n", c=DT)
        wvl_v = kA[1][:, :].rearrange("p (c n) -> p c n", c=DT)
        wv_raw = p_f[:, 0:4, :].rearrange("p r n -> p (r n)").rearrange("p (c n) -> p c n", c=DT)
        bv_all = p_f[:, 0:2, :].rearrange("p r n -> p (r n)")
        x_half = [t[:, :].rearrange("p (g t d) -> p g t d", g=2, d=D) for t in (hi_st, lo_st)]
        x_src = x.rearrange("b (g t p) d -> b g p t d", p=P, t=TB)
        wqk_src = wqk.rearrange("(c p) h m -> h p c m", p=P)
        wv_src = Wv.rearrange("(c p) n -> p c n", p=P)
        v_dst = v_scratch.rearrange("b (a h) p t c -> b a t p h c", a=2)
        out_dst = scratch.rearrange("b (n t p) (h k) -> b h n p t k", p=P, t=TB, k=K)
        hi_w = hi_st[:, :].bitcast(F32R)
        lo_w = lo_st[:, :].bitcast(F32R)

        def side_items(u, last, n):
            maxima, chunks = [[] for _ in range(STEPS)], [[] for _ in range(STEPS)]
            for t in range(STEPS):
                j, kt = divmod(t, KT)
                ahead = 0 if j < NB - 2 else 1
                if not (last and u == 1 and ahead):
                    maxima[t].append((ahead, (j + 2) % NB, kt, n))
                    n += 1
                if not last and ahead and kt in CHUNKS_AT:
                    chunks[t].append((2 * (j - NB + 2) + CHUNKS_AT.index(kt), n))
                    n += 1
            return maxima, chunks, n

        def walk(eng, prologue, head):
            with eng.Fori(0, B) as b:
                prologue(b)
                def pair(i, first, last):
                    g = eng.snap(b * H + i)
                    n = 0
                    for u in range(2):
                        n = head(b, i, g, u, first, last, n)

                pair(0, True, False)
                with eng.Fori(1, HH - 1) as k:
                    pair(eng.snap(k * 2), False, False)
                pair(H - 2, False, True)

        block = ctx.enter_context(nc.Block())

        @block.sync
        def _(sp):
            sp.sem_inc(slot_full, 16)
            for u in range(2):
                sp.sem_inc(max_row[u], 16)
                sp.sem_inc(ctx_out[u], 16)
                sp.sem_inc(v_kept[u], 16)
            sp.dma_start(ident[:, :], ident_in).then_inc(const_in, 16)
            sp.dma_start(bias[:, :], bqk).then_inc(const_in, 16)

            def load_w(hd, g):
                sp.wait_ge(w_split, g + 1)
                sp.dma_start(w_raw[:, :, :], wqk_src[bass.ds(hd, 1)]).then_inc(w_in, 16)

            def fill(u, g):
                sp.wait_ge(staged, (g + 1) * NB + 1)
                for dst, src in ((qA[u][0:K], hi_st[0:K]), (qA[u][K:P], lo_st[0:K]),
                                 (kA[u][0:K], hi_st[K:P]), (kA[u][K:P], hi_st[K:P]),
                                 (qB[u][0:K], hi_st[0:K]), (kB[u][0:K], lo_st[K:P])):
                    sp.dma_start(dst.bitcast(F32), src).then_inc(slot_full, 16)

            def load_v(b, hd, u):
                sp.dma_start(V[u][:, :, :], v_scratch[bass.ds(b, 1), bass.ds(hd, 1)]).then_inc(v_full[u], 16)

            def max_row_in(u, blk, n):
                sp.wait_ge(negm_ready, n + 1)
                dst = qB[u][K:K + 1, blk * BLK:(blk + 1) * BLK].rearrange("o (p t) -> o p t", t=TB)
                sp.dma_start(dst.bitcast(F32), negm[:, blk % 2, :].bitcast(F32)).then_inc(max_row[blk % 2], 16)

            def prologue(b):
                g = sp.snap(b * H)
                sp.wait_ge(slot_full, g * 96 + 16)
                for k in range(NB):
                    sp.dma_start(x_half[k // 2][:, k % 2], x_src[bass.ds(b, 1), k]).then_inc(x_in, 16)
                load_w(0, g)
                sp.wait_ge(pv_done, g * STEPS + PROBS)
                sp.dma_start(wv_raw, wv_src).then_inc(wv_in, 16)
                fill(0, g)
                load_w(1, g + 1)
                sp.wait_ge(wv_ready, b + 1)
                sp.dma_start(bv_all, bv.rearrange("(o n) -> o n", o=1).to_broadcast([P, H * K])).then_inc(bv_in, 16)
                for k in range(KT * 2):
                    sp.wait_ge(v_ready, b * KT * 2 + k + 1)
                    sp.dma_start(v_dst[bass.ds(b, 1), k % 2, k // 2], v_new[:, k % 2]).then_inc(v_kept[k % 2], 16)
                for u in range(2):
                    sp.wait_ge(v_kept[u], b * KT * 16 + KT * 16 + 16)
                load_v(b, 0, 0)
                max_row_in(0, 0, g * NB)
                max_row_in(0, 1, g * NB + 1)

            def head(b, i, g, u, first, last, n):
                if not (last and u == 1):
                    sp.wait_ge(pv_done, (g + u) * STEPS + PROBS)
                    fill(1 - u, g + u + 1)
                    load_v(b, i + u + 1, 1 - u)
                if not last:
                    load_w(i + u + 2, g + u + 2)
                for j in range(NB):
                    ahead = 0 if j < NB - 2 else 1
                    if not (last and u == 1 and ahead):
                        max_row_in((u + ahead) % 2, (j + 2) % NB, (g + u) * NB + j + 2)
                    sp.wait_ge(ctx_ready, (g + u) * NB + j + 1)
                    sp.dma_start(out_dst[bass.ds(b, 1), bass.ds(i + u, 1), j],
                                 ctx_n[:, j % 2]).then_inc(ctx_out[j % 2], 16)
                return n

            walk(sp, prologue, head)
            for u in range(2):
                sp.wait_ge(ctx_out[u], (B * H * NB // 2 + 1) * 16)

        @block.gpsimd
        def _(pool):
            pool.sem_inc(staged, 1)
            for u in range(2):
                nc.gpsimd.memset(kB[u][K:K + 1, :].bitcast(F32), 1.0).then_inc(ones_set, 1)
                pool.wait_ge(ones_set, u + 1)

            def low_chunk(g, chunk):
                pool.wait_ge(hi_ready, g * NB + chunk + 1)
                cols = slice(chunk * BLK, (chunk + 1) * BLK)
                nc.gpsimd.tensor_tensor(lo_w[:, cols], qk_new[:, :], hi_st[:, cols], ALU.subtract)\
                    .then_inc(staged, 1)

            def prologue(b):
                for u in range(2):
                    for c in range(NB):
                        low_chunk(b * H + u, c)

            def head(b, i, g, u, first, last, n):
                _, chunks, n = side_items(u, last, n)
                for t in range(STEPS):
                    if not lo_on_dve(t):
                        r = t % PROBS
                        pool.wait_ge(exp_done, (g + u) * STEPS + t + 1 + RING)
                        nc.gpsimd.tensor_tensor(p_l[:, r], p_f[:, r], p_h[:, r], ALU.subtract).then_inc(lo_pool, 1)
                    for chunk, _ in chunks[t - AHEAD] if t >= AHEAD else ():
                        low_chunk(g + u + 2, chunk)
                return n

            walk(pool, prologue, head)

        @block.scalar
        def _(act):
            act.sem_inc(exp_done, RING)
            act.sem_inc(ctx_free, 1)

            def copy_sums(nb):
                act.wait_ge(pv_done, (nb + 1) * KT + PROBS)
                act.wait_ge(ev_step, nb * 2 + 2)
                nc.scalar.activation(sums[:, :, :], ps_ctx[:, :, 0:2 * VW], ACT.Copy).then_inc(ctx_free, 1)

            def take_chunk(g, chunk, n, bank):
                if chunk == 0:
                    act.wait_ge(w_split, g + 2)
                act.wait_ge(staged, g * NB + chunk + 1)
                act.wait_ge(aux_full, n + 1)
                nc.scalar.activation(qk_new[:, :], ps_aux[:, bank], ACT.Identity, bias=b_cur[:, 0:1])\
                    .then_inc(qk_ready, 1)

            def prologue(b):
                g0 = act.snap(b * H)
                a0 = act.snap(g0 * AUX)
                for k in range(NB * DT):
                    g, c = divmod(k, DT)
                    act.wait_ge(pro_full, b * PRO + k + 1)
                    nc.scalar.activation(xTh[:, c, g * BLK:(g + 1) * BLK], ps_score[:, k % RING], ACT.Copy)\
                        .then_inc(xh_ready, 1)
                for c in range(NB):
                    take_chunk(g0, c, a0 + c, c % 2)
                act.wait_ge(wv_in, b * 16 + 16)
                nc.scalar.activation(wvh_v, wv_raw, ACT.Copy).then_inc(wvh_ready, 1)
                for k in range(KT * 2):
                    act.wait_ge(pro_free, b * PRO + NB * DT + k + 1 + RING)
                    vf = p_f[:, 2 + k % 2].rearrange("p (h k) -> p h k", k=K)
                    act.wait_ge(v_kept[k % 2], b * KT * 16 + k // 2 * 16 + 16)
                    nc.scalar.activation(v_new[:, k % 2, :, 0:K], vf, ACT.Copy).then_inc(vh_ready, 1)
                    act.wait_ge(vd_ready, b * KT * 2 + k + 1)
                    nc.scalar.activation(v_new[:, k % 2, :, K + 1:VW], vf, ACT.Copy, scale=LO_SCALE).then_inc(v_ready, 1)
                for c in range(NB):
                    take_chunk(g0 + 1, c, a0 + NB + c, c % 2)

            def head(b, i, g, u, first, last, n):
                _, chunks, n = side_items(u, last, n)
                for t in range(STEPS):
                    r, bank = t % PROBS, t % RING
                    act.wait_ge(s_full, (g + u) * STEPS + t + 1)
                    act.wait_ge(pv_done, (g + u) * STEPS + t + 1)
                    nc.scalar.activation(p_f[:, r], ps_score[:, bank], ACT.Exp, scale=K ** -0.5)
                    nc.scalar.activation(p_h[:, r], ps_score[:, bank], ACT.Exp, scale=K ** -0.5).then_inc(exp_done, 1)
                    for chunk, k in chunks[t - AHEAD] if t >= AHEAD else ():
                        take_chunk(g + u + 2, chunk, g * AUX + PRO_AUX + k, k % 2)
                    if t % KT == SUMS_AT and not (first and u == 0 and t < KT):
                        copy_sums((g + u) * NB + t // KT - 1)
                if last and u == 1:
                    copy_sums((g + u) * NB + NB - 1)
                return n

            walk(act, prologue, head)

        @block.vector
        def _(dve):
            dve.sem_inc(pro_free, RING)
            dve.sem_inc(max_read, 2)
            dve.sem_inc(ev_step, 2)
            dve.sem_inc(w_split, 1)
            nc.vector.memset(v_new[:, :, :, K:K + 1], 1.0)
            dve.wait_ge(const_in, 32)

            def split_w(hd, g):
                dve.wait_ge(staged, g * NB + 1)
                nc.vector.tensor_copy(b_cur[:, :], bias[:, bass.ds(hd, 1)])
                dve.wait_ge(w_in, g * 16 + 16)
                nc.vector.tensor_copy(w_h[:, :, :], w_raw[:, :, :]).then_inc(wh_ready, 1)
                dve.wait_ge(wh_ready, g + 1)
                nc.vector.tensor_tensor(w_l[:, :, :], w_raw[:, :, :], w_h[:, :, :].bitcast(F32),
                                        ALU.subtract).then_inc(w_split, 1)

            def high_chunk(g, chunk):
                cols = slice(chunk * BLK, (chunk + 1) * BLK)
                if chunk == 0:
                    dve.wait_ge(slot_full, g * 96 + 16)
                dve.wait_ge(qk_ready, g * NB + chunk + 1)
                nc.vector.tensor_copy(hi_w[:, cols], qk_new[:, :]).then_inc(hi_ready, 1)

            def maximum(hd, blk, kt, n, m, bank):
                tt, ch = divmod(kt, NB)
                dve.wait_ge(aux_full, n + 1)
                nc.vector.reduce_max(mx[:, blk % 2, tt, ch:ch + 1], ps_aux[:, bank], AX_X).then_inc(max_read, 1)
                if kt == KT - 1:
                    dve.wait_ge(max_read, m + 1 + 2)
                    nc.vector.reduce_max(mrow[:, blk % 2], mx[:, blk % 2], AX_X).then_inc(max_step, 1)

            def negate(hd, blk):
                dve.wait_ge(max_step, hd * NB + blk + 1)
                dve.wait_ge(max_row[blk % 2], (hd * (NB // 2) + blk // 2) * 16 + 16)
                nc.vector.tensor_scalar(negm[:, blk % 2], mrow[:, blk % 2], -1.0, P_SHIFT * K ** 0.5,
                                        ALU.mult, ALU.add).then_inc(negm_ready, 1)

            def low(hd, t):
                if lo_on_dve(t):
                    r = t % PROBS
                    dve.wait_ge(exp_done, hd * STEPS + t + 1 + RING)
                    nc.vector.tensor_tensor(p_l[:, r], p_f[:, r], p_h[:, r], ALU.subtract).then_inc(lo_dve, 1)

            def add_sums(nb):
                dve.wait_ge(ctx_free, nb + 2)
                acc = sums[:, :, :].rearrange("p a (t c) -> p (a t) c", c=VW)
                nc.vector.scalar_tensor_tensor(out=ctx_u[:, :, :], in0=acc[:, :, K + 1:VW], scalar=1.0 / LO_SCALE,
                                               in1=acc[:, :, 0:K], op0=ALU.mult, op1=ALU.add).then_inc(ev_step, 1)
                nc.vector.reciprocal(rden[:, :], acc[:, :, K]).then_inc(ev_step, 1)

            def divide(j, nb):
                dve.wait_ge(ev_step, nb * 2 + 4)
                dve.wait_ge(ctx_out[j % 2], (nb - j) * 8 + j // 2 * 16 + 16)
                nc.vector.tensor_tensor(ctx_n[:, j % 2], ctx_u[:, :, :],
                                        rden[:, :].unsqueeze(2).to_broadcast([P, TB, K]), ALU.mult)\
                    .then_inc(ctx_ready, 1)

            def prologue(b):
                g0 = dve.snap(b * H)
                a0 = dve.snap(g0 * AUX)
                dve.wait_ge(x_in, b * 64 + 64)
                for k in range(NB):
                    xg = x_half[k // 2][:, k % 2]
                    norm(nc, dve, xg, xg, EPS_LN, small, ln_step, (b * NB + k) * NORM)
                    nc.vector.tensor_copy(x_mean[:, bass.ds(b * NB + k, 1)], mv[:, :, 0].unsqueeze(1))
                    nc.vector.tensor_copy(x_root[:, bass.ds(b * NB + k, 1)], small[3][:, :].unsqueeze(1))
                for k in range(NB * DT):
                    gr, c = divmod(k, DT)
                    dve.wait_ge(xh_ready, b * NB * DT + k + 1)
                    cols = slice(gr * BLK, (gr + 1) * BLK)
                    nc.vector.tensor_tensor(xTl[:, c, cols], ps_score[:, k % RING], xTh[:, c, cols].bitcast(F32),
                                            ALU.subtract).then_inc(pro_free, 1)
                split_w(0, g0)
                for c in range(NB):
                    high_chunk(g0, c)
                dve.wait_ge(wvh_ready, b + 1)
                nc.vector.tensor_tensor(wvl_v, wv_raw, wvh_v.bitcast(F32), ALU.subtract).then_inc(wv_ready, 1)
                split_w(1, g0 + 1)
                dve.wait_ge(bv_in, b * 16 + 16)
                for k in range(KT * 2):
                    half = k % 2
                    dve.wait_ge(pro_full, b * PRO + NB * DT + k + 1)
                    if k >= 2:
                        dve.wait_ge(v_ready, b * KT * 2 + k - 1)
                    vf = p_f[:, 2 + k % 2]
                    nc.vector.tensor_tensor(vf, ps_score[:, k % RING], bv_all[:, half * BLK:(half + 1) * BLK],
                                            ALU.add).then_inc(pro_free, 1)
                    dve.wait_ge(vh_ready, b * KT * 2 + k + 1)
                    vf3 = vf.rearrange("p (h k) -> p h k", k=K)
                    nc.vector.tensor_tensor(vf3, vf3, v_new[:, k % 2, :, 0:K],
                                            ALU.subtract).then_inc(vd_ready, 1)
                for c in range(NB):
                    high_chunk(g0 + 1, c)
                for blk in range(2):
                    for kt in range(KT):
                        maximum(g0, blk, kt, a0 + 2 * NB + blk * KT + kt, g0 * STEPS + blk * KT + kt, kt % 2)
                    negate(g0, blk)
                for t in range(LO_AHEAD):
                    low(g0, t)

            def head(b, i, g, u, first, last, n):
                maxima, chunks, n = side_items(u, last, n)
                for t in range(STEPS):
                    j, kt = divmod(t, KT)
                    if t + LO_AHEAD < STEPS:
                        low(g + u, t + LO_AHEAD)
                    elif not (last and u == 1):
                        low(g + u + 1, t + LO_AHEAD - STEPS)
                    for ahead, blk, k, number in maxima[t]:
                        maximum(g + u + ahead, blk, k, g * AUX + PRO_AUX + number,
                                (g + u) * STEPS + 2 * KT + t, number % 2)
                    for chunk, _ in chunks[t - CHUNK_LAG] if t >= CHUNK_LAG else ():
                        high_chunk(g + u + 2, chunk)
                    block_before = not (first and u == 0 and j == 0)
                    if kt == 2 and block_before:
                        add_sums((g + u) * NB + j - 1)
                    if kt == 4 and block_before:
                        divide((j - 1) % NB, (g + u) * NB + j - 1)
                    if kt == 0 and j > 0 and maxima[t - 1]:
                        ahead, blk, _, _ = maxima[t - 1][0]
                        negate(g + u + ahead, blk)
                    if t == KT + 8 and not last:
                        split_w(i + u + 2, g + u + 2)
                if maxima[STEPS - 1]:
                    negate(g + u + 1, 1)
                if last and u == 1:
                    add_sums((g + u) * NB + NB - 1)
                    divide(NB - 1, (g + u) * NB + NB - 1)
                return n

            walk(dve, prologue, head)

        @block.tensor
        def _(pe):
            pe.sem_inc(pv_done, PROBS)
            pe.wait_ge(const_in, 32)
            pe.wait_ge(ones_set, 2)

            used = []

            def after_maxima(m):
                used[:] = [(max_read, m + 1), (max_read, m + 2)]

            def project(g, chunk, bank):
                if chunk == 0:
                    pe.wait_ge(w_split, g + 2)
                pe.wait_ge(*used.pop(0))
                used.append((qk_ready, g * NB + chunk + 1))
                cols = slice(chunk * BLK, (chunk + 1) * BLK)
                parts = [(w, t, c) for c in range(DT) for w, t in ((w_h, xTh), (w_l, xTh), (w_h, xTl))]
                for m, (w, t, c) in enumerate(parts):
                    mm = nc.tensor.matmul(ps_aux[:, bank], w[:, c], t[:, c, cols],
                                          start=(m == 0), stop=(m == len(parts) - 1))
                mm.then_inc(aux_full, 1)

            def max_tile(u, g, blk, kt, m, bank):
                tt, ch = divmod(kt, NB)
                if blk % 2 == 0 and kt == 0:
                    pe.wait_ge(slot_full, g * 96 + 96 + 16)
                pe.wait_ge(*used.pop(0))
                used.append((max_read, m + 3))
                q = qA[u][:, blk * BLK:(blk + 1) * BLK].rearrange("k (p t) -> k t p", t=TB)[:, tt]
                nc.tensor.matmul(ps_aux[:, bank], q, kA[u][:, ch * BLK:(ch + 1) * BLK],
                                 start=True, stop=True).then_inc(aux_full, 1)

            def score(u, g, t):
                j, kt = divmod(t, KT)
                if kt == 0:
                    pe.wait_ge(max_row[j % 2], (g * (NB // 2) + j // 2) * 16 + 32)
                pe.wait_ge(exp_done, g * STEPS + t + 1)
                keys, cols = slice(kt * P, (kt + 1) * P), slice(j * BLK, (j + 1) * BLK)
                nc.tensor.matmul(ps_score[:, t % RING], kA[u][:, keys], qA[u][:, cols], start=True, stop=False)
                nc.tensor.matmul(ps_score[:, t % RING], kB[u][:, keys], qB[u][:, cols],
                                 start=False, stop=True).then_inc(s_full, 1)

            def weigh(u, g, t):
                j, kt = divmod(t, KT)
                r = t % PROBS
                if kt == 0:
                    pe.wait_ge(ctx_free, (g + u) * NB + j + 1)
                if t == 0:
                    pe.wait_ge(v_full[u], g * 8 + 16)
                nd, npl = lo_counts(t)
                if lo_on_dve(t):
                    pe.wait_ge(lo_dve, (g + u) * DVE_LO + nd)
                else:
                    pe.wait_ge(lo_pool, (g + u) * POOL_LO + npl)
                for q in range(TB):
                    acc = ps_ctx[:, q // 2, (q % 2) * VW:(q % 2 + 1) * VW]
                    parts = [(p_h, VW), (p_l, K + 1)]
                    if q % 2:
                        parts.reverse()
                    for p, width in parts:
                        mm = nc.tensor.matmul(acc[:, 0:width], p[:, r, q * P:(q + 1) * P], V[u][:, kt, 0:width],
                                              start=(kt == 0 and q % 2 == 0 and p is p_h),
                                              stop=(kt == KT - 1 and q % 2 == 1 and p is p_h),
                                              skip_group_check=True)
                mm.then_inc(pv_done, 1)

            def prologue(b):
                g0 = pe.snap(b * H)
                after_maxima(g0 * STEPS)
                pe.wait_ge(exp_done, g0 * STEPS + RING)
                for k in range(NB * DT):
                    gr, c = divmod(k, DT)
                    pe.wait_ge(ln_step, (b * NB + gr + 1) * NORM)
                    pe.wait_ge(pro_free, b * PRO + k + 1)
                    xg = x_half[gr // 2][:, gr % 2]
                    for t in range(TB):
                        mm = nc.tensor.transpose(ps_score[:, k % RING, t * P:(t + 1) * P],
                                                 xg[:, t, c * P:(c + 1) * P], ident[:, :])
                    mm.then_inc(pro_full, 1)
                pe.wait_ge(pro_free, b * PRO + NB * DT + RING)
                for c in range(NB):
                    project(g0, c, c % 2)
                pe.wait_ge(wv_ready, b + 1)
                for k in range(KT * 2):
                    tt, half = divmod(k, 2)
                    pe.wait_ge(pro_free, b * PRO + NB * DT + k + 1)
                    toks, cols = slice(tt * P, (tt + 1) * P), slice(half * BLK, (half + 1) * BLK)
                    parts = [(t, w, c) for c in range(DT)
                             for t, w in ((xTh, wvh_v), (xTh, wvl_v), (xTl, wvh_v))]
                    for m, (t, w, c) in enumerate(parts):
                        mm = nc.tensor.matmul(ps_score[:, k % RING], t[:, c, toks], w[:, c, cols],
                                              start=(m == 0), stop=(m == len(parts) - 1))
                    mm.then_inc(pro_full, 1)
                for c in range(NB):
                    project(g0 + 1, c, c % 2)
                for blk in range(2):
                    for kt in range(KT):
                        max_tile(0, g0, blk, kt, g0 * STEPS + blk * KT + kt, kt % 2)
                pe.wait_ge(pro_free, b * PRO + PRO + RING)
                for t in range(AHEAD):
                    score(0, g0, t)

            def head(b, i, g, u, first, last, n):
                maxima, chunks, n = side_items(u, last, n)
                if u == 0:
                    after_maxima(g * STEPS + 2 * KT)
                for t in range(STEPS):
                    j, kt = divmod(t, KT)
                    for ahead, blk, k, number in maxima[t]:
                        max_tile((u + ahead) % 2, g + u + ahead, blk, k, (g + u) * STEPS + 2 * KT + t, number % 2)
                    if t + AHEAD < STEPS:
                        score(u, g + u, t + AHEAD)
                    elif not (last and u == 1):
                        score(1 - u, g + u + 1, t + AHEAD - STEPS)
                    if t % 2:
                        weigh(u, g, t - 1)
                        for chunk, number in chunks[t]:
                            project(g + u + 2, chunk, number % 2)
                        weigh(u, g, t)
                return n

            walk(pe, prologue, head)


def feed_forward(nc, x, scratch, Wo, bo, gamma, beta, wgT, wuT, wdT, ident_in, out, x_mean, x_root):
    B, S, D = x.shape
    HK = Wo.shape[0]
    F = wgT.shape[1]
    DT, CT, FT = D // P, HK // P, F // P
    TB = BLK // P
    G = B * S // BLK
    FEED = CT + DT
    TURN = FEED + 2 * DT
    CHAIN = 3 * ROOT + 4
    assert DT == 2 and TB == 4 and CT % 2 == 0 and FT % 2 == 0 and G % 2 == 0 and G >= 4

    def turn_base(g):
        if isinstance(g, int) and g == G - 1:
            return 2 * FEED + (G - 2) * TURN + 2 * DT
        return g * TURN + 2 * FEED

    def feed_at(f):
        return range(f * CT // FT, (f + 1) * CT // FT)

    with ExitStack() as ctx:
        sb = lambda n, s, d: ctx.enter_context(nc.sbuf_tensor(n, s, d))
        sem = lambda n: ctx.enter_context(nc.semaphore(n))
        bank = lambda n, k: ctx.enter_context(nc.psum_tensor(n, [P, k, BLK], F32))
        ps_t = bank("ps_t", 2)
        ps_y = bank("ps_y", 2)
        ps_g = bank("ps_g", 2)
        ps_u = bank("ps_u", 2)

        id2 = sb("id2", [P, P], F32)
        bo_c = sb("bo_c", [P, DT], F32)
        gam = sb("gam", [P, D], F32)
        bet = sb("bet", [P, D], F32)
        raw = sb("raw", [P, DT * F], I32)
        wo = [sb(f"wo{m}", [P, CT, D], F32R) for m in "hl"]
        wg = [sb(f"wg{m}", [P, DT, F], F32R) for m in "hl"]
        wu = [sb(f"wu{m}", [P, DT, F], F32R) for m in "hl"]
        wd = [sb(f"wd{m}", [P, FT, D], F32R) for m in "hl"]
        c_in = sb("c_in", [P, TB, HK], F32)
        x_t = [sb(f"x_t{u}", [P, TB, D], F32) for u in range(2)]
        cT = [sb(f"cT{m}", [P, CT, BLK], F32R) for m in "hl"]
        yT = sb("yT", [P, DT, BLK], F32)
        xn = sb("xn", [P, TB, D], F32)
        z = sb("z", [P, TB, D], F32)
        late = sb("late", [P, 5, TB * D], F32)
        tokens = lambda n: late[:, n].rearrange("p (t d) -> p t d", t=TB)
        halves = lambda n: late[:, n].rearrange("p (c n) -> p c n", c=DT)
        sg, hf, oT = halves(0), halves(1), halves(2)
        o_tok = tokens(3)
        x1 = [sb("x1_0", [P, TB, D], F32), tokens(4)]
        xn2 = sb("xn2", [P, TB, D], F32)
        nT = [sb(f"nT{m}", [P, DT, BLK], F32R) for m in "hl"]
        hT = [sb(f"hT{m}", [P, FT, BLK], F32R) for m in "hl"]
        st2 = sb("st2", [P, TB, 6], F32)
        mv2 = sb("mv2", [P, TB, 2], F32)
        small = (st2, mv2, *(sb(f"norm2_{k}", [P, TB], F32) for k in range(3)))

        const_loaded = sem("const_loaded")
        w_loaded = [sem(f"w_loaded{k}") for k in range(4)]
        w_float = sem("w_float")
        w_hi = sem("w_hi")
        w_parts = sem("w_parts")
        c_loaded = sem("c_loaded")
        x_loaded = [sem(f"x_loaded{u}") for u in range(2)]
        x_used = sem("x_used")
        centred = sem("centred")
        xn_ready = sem("xn_ready")
        t_full = sem("t_full")
        t_free = sem("t_free")
        c_hi = sem("c_hi")
        y_full = sem("y_full")
        y_read = sem("y_read")
        chain_step = sem("chain_step")
        n_hi = sem("n_hi")
        g_full = sem("g_full")
        silu_done = sem("silu_done")
        u_full = sem("u_full")
        h_ready = sem("h_ready")
        h_hi = sem("h_hi")
        h_lo = sem("h_lo")
        o_full = sem("o_full")
        o_read = sem("o_read")
        end_step = sem("end_step")
        res_ready = sem("res_ready")
        stored = [sem(f"stored{u}") for u in range(2)]

        xv = x.rearrange("b (g t p) d -> (b g) p t d", p=P, t=TB)
        ov = out.rearrange("b (g t p) d -> (b g) p t d", p=P, t=TB)
        cv = scratch.rearrange("b (g t p) n -> (b g) p t n", p=P, t=TB)
        flat = late[:, :, :].rearrange("p a n -> p (a n)")
        cut = lambda a, c, n: flat[:, a:a + c * n].rearrange("p (c n) -> p c n", c=c)
        stage_o = cut(0, CT, D)
        stage_g = cut(CT * D, DT, F).bitcast(I32)
        stage_d = cut(CT * D + DT * F, FT, D).bitcast(I32)
        stage_u = raw[:, :].rearrange("p (c n) -> p c n", c=DT)
        assert CT * D + 2 * DT * F <= 5 * TB * D
        weights = [(Wo.rearrange("(c p) n -> p c n", p=P), stage_o, wo),
                   (wgT.rearrange("(c p) n -> p c n", p=P), stage_g, wg),
                   (wuT.rearrange("(c p) n -> p c n", p=P), stage_u, wu),
                   (wdT.rearrange("(c p) n -> p c n", p=P), stage_d, wd)]

        def walk(eng, feed, chain, turn, end):
            feed(0, 0)
            feed(1, 1)
            chain(0, 0)
            turn(0, 0, True, True, True)
            with eng.Fori(0, (G - 4) // 2) as i:
                g = eng.snap(i * 2 + 1)
                turn(g, 1, False, True, True)
                turn(g + 1, 0, False, True, True)
            turn(G - 3, 1, False, True, True)
            turn(G - 2, 0, False, False, True)
            turn(G - 1, 1, False, False, False)
            end(G - 1, 1)

        nothing = lambda g, u: None
        block = ctx.enter_context(nc.Block())

        @block.sync
        def _(sp):
            row = lambda v: v.rearrange("(o n) -> o n", o=1).to_broadcast([P, D])

            def load_c(g, transposed):
                if transposed is not None:
                    sp.wait_ge(t_full, transposed)
                sp.dma_start(c_in[:, :, :], cv[bass.ds(g, 1)]).then_inc(c_loaded, 16)

            def load_x(g, u):
                sp.wait_ge(x_used, g + 1)
                sp.dma_start(x_t[u][:, :, :], xv[bass.ds(g, 1)]).then_inc(x_loaded[u], 16)

            def load_w(k):
                src, stage, _ = weights[k]
                sp.dma_start(stage, src).then_inc(w_loaded[k], 16)

            def store(g, u):
                sp.wait_ge(res_ready, g + 2)
                sp.dma_start(ov[bass.ds(g, 1)], x1[u][:, :, :]).then_inc(stored[u], 16)

            for u in range(2):
                sp.sem_inc(stored[u], 16)
            sp.dma_start(id2[:, :], ident_in).then_inc(const_loaded, 16)
            load_c(0, None)
            load_w(0)
            sp.dma_start(bo_c[:, :], bo).then_inc(const_loaded, 16)
            load_x(0, 0)
            load_x(1, 1)
            sp.dma_start(gam[:, :], row(gamma)).then_inc(const_loaded, 16)
            sp.dma_start(bet[:, :], row(beta)).then_inc(const_loaded, 16)
            load_c(1, CT)
            for k in range(1, 4):
                load_w(k)
            load_c(2, FEED + CT)
            load_x(2, 0)

            def turn(g, u, first, feeds, chains):
                if not first:
                    store(g - 1, 1 - u)
                if feeds and not (isinstance(g, int) and g == G - 3):
                    load_c(g + 3, turn_base(g) + DT + CT)
                    load_x(g + 3, 1 - u)

            walk(sp, nothing, nothing, turn, store)
            for u in range(2):
                sp.wait_ge(stored[u], 16 * (G // 2 + 1))

        @block.scalar
        def _(act):
            act.sem_inc(o_read, 3 * DT)
            act.sem_inc(silu_done, 2)

            def hi_c(g, k, item):
                act.wait_ge(t_full, item + 1)
                nc.scalar.activation(cT[0][:, k], ps_t[:, k % 2], ACT.Copy).then_inc(c_hi, 1)

            def copy_y(g):
                for c in range(DT):
                    act.wait_ge(y_full, g * DT + c + 1)
                    nc.scalar.activation(yT[:, c], ps_y[:, c], ACT.Identity, bias=bo_c[:, c:c + 1])\
                        .then_inc(y_read, 1)

            def prepare(k):
                _, stage, parts = weights[k]
                act.wait_ge(w_loaded[k], 16)
                if k:
                    nc.scalar.activation(stage.bitcast(F32), stage, ACT.Copy, scale=1.0 / 127.0).then_inc(w_float, 1)
                    act.wait_ge(w_float, k)
                nc.scalar.activation(parts[0][:, :, :], stage.bitcast(F32) if k else stage, ACT.Copy).then_inc(w_hi, 1)

            def feed(g, u):
                if g == 0:
                    act.wait_ge(const_loaded, 64)
                    prepare(0)
                for k in range(CT):
                    hi_c(g, k, g * FEED + k)
                copy_y(g)
                if g == 0:
                    for k in range(1, 4):
                        prepare(k)

            def turn(g, u, first, feeds, chains):
                base = turn_base(g)
                for c in range(DT):
                    act.wait_ge(t_full, base + c + 1)
                    nc.scalar.activation(nT[0][:, c], ps_t[:, c], ACT.Copy).then_inc(n_hi, 1)

                def hi_h(f):
                    act.wait_ge(h_ready, g * FT + f + 3)
                    nc.scalar.activation(hT[0][:, f], hf[:, f % 2], ACT.Copy).then_inc(h_hi, 1)

                act.wait_ge(o_full, g * DT + DT)
                for f in range(FT):
                    act.wait_ge(g_full, g * FT + f + 1)
                    act.wait_ge(h_ready, g * FT + f + 1)
                    nc.scalar.activation(sg[:, f % 2], ps_g[:, f % 2], ACT.Silu).then_inc(silu_done, 1)
                    if feeds:
                        for k in feed_at(f):
                            hi_c(g + 2, k, base + DT + k)
                    if f:
                        hi_h(f - 1)
                hi_h(FT - 1)
                if feeds:
                    copy_y(g + 2)
                for c in range(DT):
                    act.wait_ge(o_full, g * DT + c + 1 + DT)
                    nc.scalar.activation(oT[:, c], ps_y[:, c], ACT.Copy).then_inc(o_read, 1)

            walk(act, feed, nothing, turn, nothing)

        @block.gpsimd
        def _(pool):
            pool.sem_inc(h_lo, 2)
            pool.sem_inc(res_ready, 1)

            def norm_x(g, u):
                if not (isinstance(g, int) and g == 0):
                    pool.wait_ge(chain_step, (g - 1) * CHAIN + 1)
                pool.wait_ge(x_loaded[u], (g - u) * 8 + 16)
                stat = lambda v: v[:, bass.ds(g, 1)].rearrange("p o t -> p (o t)").unsqueeze(2)\
                    .to_broadcast([P, TB, D])
                nc.gpsimd.tensor_tensor(xn[:, :, :], x_t[u][:, :, :], stat(x_mean), ALU.subtract)\
                    .then_inc(centred, 1)
                pool.wait_ge(centred, g + 1)
                nc.gpsimd.tensor_tensor(xn[:, :, :], xn[:, :, :], stat(x_root), ALU.mult).then_inc(xn_ready, 1)

            def residual(g, u):
                pool.wait_ge(end_step, (g + 1) * NORM)
                nc.gpsimd.tensor_tensor(x1[u][:, :, :], x1[u][:, :, :], o_tok[:, :, :], ALU.add)\
                    .then_inc(res_ready, 1)

            def turn(g, u, first, feeds, chains):
                for f in range(FT):
                    pool.wait_ge(h_hi, g * FT + f + 1)
                    nc.gpsimd.tensor_tensor(hT[1][:, f], hf[:, f % 2], hT[0][:, f].bitcast(F32),
                                            ALU.subtract).then_inc(h_lo, 1)
                    if f == 1 and not first:
                        residual(g - 1, 1 - u)
                if feeds:
                    norm_x(g + 2, u)

            walk(pool, norm_x, nothing, turn, residual)

        @block.vector
        def _(dve):
            dve.sem_inc(t_free, 2)
            dve.sem_inc(h_ready, 2)
            dve.sem_inc(x_used, 2)
            dve.wait_ge(const_loaded, 64)

            def prepare(k):
                _, stage, parts = weights[k]
                dve.wait_ge(w_hi, k + 1)
                nc.vector.tensor_tensor(parts[1][:, :, :], stage.bitcast(F32) if k else stage, parts[0][:, :, :].bitcast(F32),
                                        ALU.subtract).then_inc(w_parts, 1)

            def lo_c(g, k):
                dve.wait_ge(c_hi, g * CT + k + 1)
                nc.vector.tensor_tensor(cT[1][:, k], ps_t[:, k % 2], cT[0][:, k].bitcast(F32),
                                        ALU.subtract).then_inc(t_free, 1)

            def add_x(g, item):
                dve.wait_ge(xn_ready, g + 1)
                for c in range(2):
                    dve.wait_ge(t_full, item + c + 1)
                    half = slice(2 * c, 2 * c + 2)
                    nc.vector.tensor_tensor(z[:, half], ps_t[:, c].rearrange("p (t d) -> p t d", d=D), xn[:, half],
                                            ALU.add).then_inc(t_free, 1)
                dve.wait_ge(t_free, item + 2 + 2)

            _, mv, _, y, _ = small
            col = lambda t: (mv[:, t, 0:1], y[:, t:t + 1])

            def root_z(g, u):
                root(nc, dve, z, EPS_ATTN, small, chain_step, g * CHAIN)

            def gamma_beta(g, u):
                for t in range(TB):
                    ins = nc.vector.scalar_tensor_tensor(out=z[:, t], in0=z[:, t], scalar=col(t)[0], in1=gam[:, :],
                                                         op0=ALU.subtract, op1=ALU.mult)
                ins.then_inc(chain_step, 1)
                dve.wait_ge(chain_step, g * CHAIN + ROOT + 1)
                for t in range(TB):
                    ins = nc.vector.scalar_tensor_tensor(out=z[:, t], in0=z[:, t], scalar=col(t)[1], in1=bet[:, :],
                                                         op0=ALU.mult, op1=ALU.add)
                ins.then_inc(chain_step, 1)
                dve.wait_ge(chain_step, g * CHAIN + ROOT + 2)

            def root_again(g, u):
                root(nc, dve, z, EPS_LN, small, chain_step, g * CHAIN + ROOT + 2)

            def first_residual(g, u):
                for t in range(TB):
                    ins = nc.vector.tensor_scalar(z[:, t], z[:, t], *col(t), ALU.subtract, ALU.mult)
                ins.then_inc(chain_step, 1)
                dve.wait_ge(chain_step, g * CHAIN + 2 * ROOT + 3)
                dve.wait_ge(stored[u], (g - u) * 8 + 16)
                nc.vector.tensor_tensor(x1[u][:, :, :], x_t[u][:, :, :], z[:, :, :], ALU.add).then_inc(x_used, 1)
                dve.wait_ge(x_used, g + 3)

            def norm_x1(g, u):
                norm(nc, dve, xn2, x1[u], EPS_LN, small, chain_step, g * CHAIN + 2 * ROOT + 3)

            def last_norm(g, u):
                norm(nc, dve, o_tok, o_tok, EPS_LN, small, end_step, g * NORM)

            def feed(g, u):
                if g == 0:
                    prepare(0)
                for k in range(CT):
                    lo_c(g, k)
                if g == 0:
                    add_x(0, CT)
                    for k in range(1, 4):
                        prepare(k)

            def chain(g, u):
                for piece in (root_z, gamma_beta, root_again, first_residual, norm_x1):
                    piece(g, u)
                add_x(1, FEED + CT)

            def turn(g, u, first, feeds, chains):
                base = turn_base(g)
                for c in range(DT):
                    dve.wait_ge(n_hi, g * DT + c + 1)
                    nc.vector.tensor_tensor(nT[1][:, c], ps_t[:, c], nT[0][:, c].bitcast(F32),
                                            ALU.subtract).then_inc(t_free, 1)
                for f in range(FT):
                    dve.wait_ge(u_full, g * FT + f + 1)
                    dve.wait_ge(silu_done, g * FT + f + 3)
                    dve.wait_ge(h_lo, g * FT + f + 1)
                    nc.vector.tensor_tensor(hf[:, f % 2], ps_u[:, f % 2], sg[:, f % 2], ALU.mult)\
                        .then_inc(h_ready, 1)
                    if feeds:
                        for k in feed_at(f):
                            lo_c(g + 2, k)
                    if f == 0 and not first:
                        last_norm(g - 1, 1 - u)
                    if f == 1 and chains:
                        root_z(g + 1, 1 - u)
                    if f == 2 and chains:
                        gamma_beta(g + 1, 1 - u)
                    if f == 3 and chains:
                        root_again(g + 1, 1 - u)
                if chains:
                    first_residual(g + 1, 1 - u)
                    norm_x1(g + 1, 1 - u)
                if feeds:
                    add_x(g + 2, base + DT + CT)
                item = base + DT + (FEED if feeds else 0)
                dve.wait_ge(res_ready, g + 1)
                for c in range(2):
                    dve.wait_ge(t_full, item + c + 1)
                    nc.vector.tensor_copy(o_tok[:, 2 * c:2 * c + 2],
                                          ps_t[:, c].rearrange("p (t d) -> p t d", d=D)).then_inc(t_free, 1)
                dve.wait_ge(t_free, item + DT + 2)

            walk(dve, feed, chain, turn, last_norm)

        @block.tensor
        def _(pe):
            pe.sem_inc(o_full, DT)
            pe.wait_ge(const_loaded, 64)

            def product(dst, terms):
                passes = [(w[m], t[k]) for w, t in terms for m, k in ((0, 0), (1, 0), (0, 1))]
                for n, (w, t) in enumerate(passes):
                    mm = nc.tensor.matmul(dst, w, t, start=(n == 0), stop=(n == len(passes) - 1))
                return mm

            def turn_back(src, item):
                for c in range(2):
                    pe.wait_ge(t_free, item + c + 1)
                    for t in range(2):
                        for w in range(DT):
                            mm = nc.tensor.transpose(ps_t[:, c, (t * DT + w) * P:(t * DT + w + 1) * P],
                                                     src[:, w, (2 * c + t) * P:(2 * c + t + 1) * P], id2[:, :])
                    mm.then_inc(t_full, 1)

            def turn_tile(bank_of, src, item):
                pe.wait_ge(t_free, item + 1)
                for t in range(TB):
                    mm = nc.tensor.transpose(ps_t[:, bank_of, t * P:(t + 1) * P], src(t), id2[:, :])
                mm.then_inc(t_full, 1)

            def turn_c(k, item):
                turn_tile(k % 2, lambda t: c_in[:, t, k * P:(k + 1) * P], item)

            def project_out(g, item):
                pe.wait_ge(t_free, item + 1 + 2)
                for c in range(DT):
                    pe.wait_ge(o_read, g * DT + c + 1)
                    product(ps_y[:, c], [([w[:, k, c * P:(c + 1) * P] for w in wo], [t[:, k] for t in cT])
                                         for k in range(CT)]).then_inc(y_full, 1)

            def feed(g, u):
                pe.wait_ge(c_loaded, g * 16 + 16)
                for k in range(CT):
                    turn_c(k, g * FEED + k)
                if g == 0:
                    pe.wait_ge(w_parts, 1)
                project_out(g, g * FEED + CT - 1)
                pe.wait_ge(y_read, g * DT + DT)
                turn_back(yT, g * FEED + CT)

            def turn(g, u, first, feeds, chains):
                base = turn_base(g)
                pe.wait_ge(chain_step, (g + 1) * CHAIN)
                for c in range(DT):
                    turn_tile(c, lambda t: xn2[:, t, c * P:(c + 1) * P], base + c)
                if first:
                    pe.wait_ge(w_parts, 4)
                pe.wait_ge(t_free, base + DT + 2)
                if feeds:
                    pe.wait_ge(c_loaded, (g + 2) * 16 + 16)
                for f in range(FT):
                    fs = slice(f * P, (f + 1) * P)
                    for ps, w, full, free in ((ps_g, wg, g_full, silu_done), (ps_u, wu, u_full, h_ready)):
                        pe.wait_ge(free, g * FT + f + 1)
                        product(ps[:, f % 2], [([v[:, c, fs] for v in w], [t[:, c] for t in nT])
                                               for c in range(DT)]).then_inc(full, 1)
                    if feeds:
                        for k in feed_at(f):
                            turn_c(k, base + DT + k)
                if feeds:
                    project_out(g + 2, base + DT + CT - 1)
                pe.wait_ge(h_lo, g * FT + FT + 2)
                for c in range(DT):
                    pe.wait_ge(y_read, (g + 2) * DT + c + 1 if feeds else G * DT)
                    if feeds and c == 1:
                        turn_back(yT, base + DT + CT)
                    if not feeds and not chains:
                        pe.wait_ge(o_read, g * DT + c + 1 + 2 * DT)
                    product(ps_y[:, c], [([w[:, f, c * P:(c + 1) * P] for w in wd], [t[:, f] for t in hT])
                                         for f in range(FT)]).then_inc(o_full, 1)
                pe.wait_ge(o_read, (g + 4) * DT)
                turn_back(oT, base + DT + (FEED if feeds else 0))

            walk(pe, feed, nothing, turn, nothing)


def program(nc, x, wqk, bqk, Wv, bv, Wo, bo, gamma, beta, wgT, wuT, wdT, ident, out):
    B, S, _ = x.shape
    scratch = nc.dram_tensor("heads", (B, S, Wo.shape[0]), F32, kind="Internal").ap()
    v_scratch = nc.dram_tensor("v_heads", (B, wqk.shape[1], P, S // P, wqk.shape[2] + 1), F16, kind="Internal").ap()
    nc.disable_value_cache = True
    groups, tiles = B * S // BLK, BLK // P
    with nc.sbuf_tensor("x_mean", [P, groups, tiles], F32) as x_mean, \
            nc.sbuf_tensor("x_root", [P, groups, tiles], F32) as x_root:
        attention(nc, x, wqk, bqk, Wv, bv, ident, v_scratch, scratch, x_mean, x_root)
        feed_forward(nc, x, scratch, Wo, bo, gamma, beta, wgT, wuT, wdT, ident, out, x_mean, x_root)


def kernel(L0_attn_x, L0_attn_Wq, L0_attn_bq, L0_attn_Wk, L0_attn_bk, L0_attn_Wv, L0_attn_bv, L0_attn_Wo,
           L0_attn_bo, L0_attn_gamma, L0_attn_beta, L0_ffn_w_gate, L0_ffn_w_up, L0_ffn_w_down):
    import numpy as np
    import concourse.bacc as bacc
    from concourse.bass_utils import run_bass_kernel_spmd

    a = lambda v: np.ascontiguousarray(v)
    D, H, K = L0_attn_Wq.shape
    arrays = {
        "x": a(L0_attn_x),
        "wqk": a(np.concatenate([L0_attn_Wq, L0_attn_Wk], axis=2)),
        "bqk": a(np.concatenate([L0_attn_bq, L0_attn_bk], axis=1).T),
        "Wv": a(np.reshape(L0_attn_Wv, (D, H * K))),
        "bv": a(np.reshape(L0_attn_bv, (H * K,))),
        "Wo": a(np.reshape(L0_attn_Wo, (H * K, D))),
        "bo": a(np.reshape(L0_attn_bo, (D // P, P)).T),
        "gamma": a(L0_attn_gamma),
        "beta": a(L0_attn_beta),
        "wgT": a(np.transpose(L0_ffn_w_gate)),
        "wuT": a(np.transpose(L0_ffn_w_up)),
        "wdT": a(np.transpose(L0_ffn_w_down)),
        "ident": np.eye(P, dtype=np.float32),
    }
    nc = bacc.Bacc("TRN2", target_bir_lowering=False, num_devices=1)
    args = [nc.dram_tensor(f"in_{n}", v.shape, mybir.dt.from_np(v.dtype), kind="ExternalInput").ap()
            for n, v in arrays.items()]
    out = nc.dram_tensor("out", arrays["x"].shape, F32, kind="ExternalOutput").ap()
    program(nc, *args, out)
    r = run_bass_kernel_spmd(nc, [{f"in_{n}": v for n, v in arrays.items()}], core_ids=[0])
    return r.results[0]["out"]
```

```python
from contextlib import ExitStack

import concourse.bass as bass
from concourse import mybir

P = 128
ALU = mybir.AluOpType
ACT = mybir.ActivationFunctionType
F32 = mybir.dt.float32
F32R = mybir.dt.float32r
F16 = mybir.dt.float16
I32 = mybir.dt.int32
AX_X = mybir.AxisListType.X

EPS_LN = 1e-5
EPS_ATTN = 1e-3
BLK = 512
RING = 4
PROBS = 8
AHEAD = 6
LO_AHEAD = 3
CHUNK_LAG = 4
P_SHIFT = 5.545177444479562
LO_SCALE = 2048.0
SUMS_AT = 4
CHUNKS_AT = (3, 9)


def lo_on_dve(t):
    return t % 8 in (1, 3, 5)


def lo_counts(t):
    dve = sum(lo_on_dve(k) for k in range(t + 1))
    return dve, t + 1 - dve


MOMENTS = 2
NEWTON = 12
ROOT = MOMENTS + NEWTON
NORM = ROOT + 1
RSQRT_SEED = float(0x5F3759DF)


def moments(nc, dve, src, small, step, value):
    stats, mv, v, _, _ = small
    for t in range(src.shape[1]):
        ins = nc.vector.bn_stats(stats[:, t], src[:, t])
    ins.then_inc(step, 1)
    dve.wait_ge(step, value + 1)
    nc.vector.memset(v[:, :], 0.0)
    for t in range(src.shape[1]):
        ins = nc.vector.bn_aggr(mv[:, t], stats[:, t])
    ins.then_inc(step, 1)
    dve.wait_ge(step, value + MOMENTS)


def newton(nc, dve, eps, small, step, value):
    _, mv, v, y, w = small
    n = [0]

    def then(ins):
        n[0] += 1
        ins.then_inc(step, 1)
        dve.wait_ge(step, value + n[0])

    then(nc.vector.tensor_scalar(v[:, :], mv[:, :, 1], eps, None, ALU.add))
    then(nc.vector.tensor_scalar(w[:, :].bitcast(I32), v[:, :].bitcast(I32), 1, None, ALU.logical_shift_right))
    then(nc.vector.tensor_scalar(y[:, :].bitcast(I32), w[:, :].bitcast(I32), -1.0, RSQRT_SEED, ALU.mult, ALU.add))
    for _ in range(3):
        then(nc.vector.tensor_tensor(w[:, :], y[:, :], y[:, :], ALU.mult))
        then(nc.vector.scalar_tensor_tensor(out=w[:, :], in0=w[:, :], scalar=-0.5, in1=v[:, :],
                                            op0=ALU.mult, op1=ALU.mult))
        then(nc.vector.scalar_tensor_tensor(out=y[:, :], in0=w[:, :], scalar=1.5, in1=y[:, :],
                                            op0=ALU.add, op1=ALU.mult))
    assert n[0] == NEWTON


def norm(nc, dve, dst, src, eps, small, step, value):
    moments(nc, dve, src, small, step, value)
    scale(nc, dve, dst, src, eps, small, step, value)


def scale(nc, dve, dst, src, eps, small, step, value):
    newton(nc, dve, eps, small, step, value + MOMENTS)
    apply_root(nc, dve, dst, src, small, step, value)


def apply_root(nc, dve, dst, src, small, step, value):
    _, mv, _, y, _ = small
    for t in range(dst.shape[1]):
        ins = nc.vector.tensor_scalar(dst[:, t], src[:, t], mv[:, t, 0:1], y[:, t:t + 1], ALU.subtract, ALU.mult)
    ins.then_inc(step, 1)
    dve.wait_ge(step, value + NORM)


def snap(eng, value):
    return value if isinstance(value, int) else eng.snap(value)


def attention(nc, x, wqk, bqk, Wv, bv, ident_in, v_scratch, scratch, Wo, shared):
    B, S, D = x.shape
    H = wqk.shape[1]
    K = wqk.shape[2] // 2
    DT = D // P
    KT = S // P
    NB = S // BLK
    TB = BLK // P
    STEPS = NB * KT
    AUX = NB + STEPS
    PRO_AUX = 2 * NB + 2 * KT
    TURNS = NB * DT
    VALUES = KT * 2
    VW = 2 * K + 1
    DVE_LO, POOL_LO = lo_counts(STEPS - 1)
    HH = H // 2
    ident, x_mean, x_root, x_all, hi_st, c_loaded, wo_loaded = shared
    assert B > 1

    with ExitStack() as ctx:
        sb = lambda n, s, d: ctx.enter_context(nc.sbuf_tensor(n, s, d))
        sem = lambda n: ctx.enter_context(nc.semaphore(n))
        ps_score = ctx.enter_context(nc.psum_tensor("ps_score", [P, RING, BLK], F32))
        ps_aux = ctx.enter_context(nc.psum_tensor("ps_aux", [P, 2, BLK], F32))
        ps_ctx = ctx.enter_context(nc.psum_tensor("ps_ctx", [P, 2, BLK], F32))

        qA = [sb(f"q_hilo{u}", [P, S], F32R) for u in range(2)]
        kA = [sb(f"k_hihi{u}", [P, S], F32R) for u in range(2)]
        qB = [sb(f"q_hi_max{u}", [K + 1, S], F32R) for u in range(2)]
        kB = [sb(f"k_lo_one{u}", [K + 1, S], F32R) for u in range(2)]
        qk_new = sb("qk_new", [P, BLK], F32)
        lo_st = sb("lo_st", [P, S], F32)
        xTh = sb("xTh", [P, DT, S], F32R)
        xTl = sb("xTl", [P, DT, S], F32R)
        v_new = sb("v_new", [P, 4, HH, VW], F16)
        V = [sb(f"v_hi_one_lo{u}", [P, KT, VW], F16) for u in range(2)]
        p_f = sb("p_f", [P, PROBS, BLK], F32)
        p_h = sb("p_h", [P, PROBS, BLK], F16)
        p_l = sb("p_l", [P, PROBS, BLK], F16)
        w_raw = sb("w_raw", [P, DT, P], F32)
        w_h = sb("w_h", [P, DT, P], F32R)
        w_l = sb("w_l", [P, DT, P], F32R)
        bias = sb("bias", [P, H], F32)
        b_cur = sb("b_cur", [P, 1], F32)
        mx = sb("mx", [P, 2, TB, NB], F32)
        mrow = sb("mrow", [P, 2, TB], F32)
        negm = sb("negm", [P, 2, TB], F32R)
        sums = sb("sums", [P, 2, 2 * VW], F32)
        rden = sb("rden", [P, TB], F32)
        ctx_u = sb("ctx_u", [P, TB, K], F32)
        ctx_n = sb("ctx_n", [P, 2, TB, K], F32)
        stats = sb("stats", [P, TB, 6], F32)
        mv = sb("mv", [P, TB, 2], F32)
        small = (stats, mv, *(sb(f"norm{k}", [P, TB], F32) for k in range(3)))

        const_in = sem("const_in")
        ones_set = sem("ones_set")
        x_in = [sem(f"x_in{k}") for k in range(NB)]
        ln_step = sem("ln_step")
        pro_full = sem("pro_full")
        pro_free = sem("pro_free")
        xh_ready = sem("xh_ready")
        x_split = sem("x_split")
        wv_in = sem("wv_in")
        wvh_ready = sem("wvh_ready")
        wv_ready = sem("wv_ready")
        bv_in = sem("bv_in")
        vh_ready = sem("vh_ready")
        vd_ready = sem("vd_ready")
        v_ready = sem("v_ready")
        v_kept = [sem(f"v_kept{r}") for r in range(4)]
        v_full = [sem(f"v_full{u}") for u in range(2)]
        w_in = sem("w_in")
        wh_ready = sem("wh_ready")
        w_split = sem("w_split")
        aux_full = sem("aux_full")
        max_read = sem("max_read")
        qk_ready = sem("qk_ready")
        hi_ready = sem("hi_ready")
        staged = sem("staged")
        slot_full = sem("slot_full")
        max_step = sem("max_step")
        negm_ready = sem("negm_ready")
        max_row = [sem(f"max_row{u}") for u in range(2)]
        s_full = sem("s_full")
        exp_done = sem("exp_done")
        lo_dve = sem("lo_dve")
        lo_pool = sem("lo_pool")
        pv_done = sem("pv_done")
        ev_step = sem("ev_step")
        ctx_free = sem("ctx_free")
        ctx_ready = sem("ctx_ready")
        ctx_out = [sem(f"ctx_out{u}") for u in range(2)]

        wvh_v = qA[1][:, :].rearrange("p (c n) -> p c n", c=DT)
        wvl_v = kA[1][:, :].rearrange("p (c n) -> p c n", c=DT)
        wv_raw = p_f[:, 0:4, :].rearrange("p r n -> p (r n)").rearrange("p (c n) -> p c n", c=DT)
        bv_all = p_f[:, 6:8, :].rearrange("p r n -> p (r n)")
        c_first = x_all[:, :, :, :].rearrange("p g t d -> p (g t d)").rearrange("p (t n) -> p t n", t=TB)
        c_src = scratch.rearrange("b (g t p) n -> (b g) p t n", p=P, t=TB)[0]
        x_src = x.rearrange("b (g t p) d -> b g p t d", p=P, t=TB)
        wqk_src = wqk.rearrange("(c p) h m -> h p c m", p=P)
        wv_src = Wv.rearrange("(c p) n -> p c n", p=P)
        v_dst = v_scratch.rearrange("b (a h) p t c -> b a t p h c", a=2)
        out_dst = scratch.rearrange("b (n t p) (h k) -> b h n p t k", p=P, t=TB, k=K)
        hi_w = hi_st[:, :].bitcast(F32R)
        lo_w = lo_st[:, :].bitcast(F32R)

        def score_base(b):
            return 0 if isinstance(b, int) and b == 0 else b * VALUES + TURNS

        def prologue_items(opening):
            order, values = [], iter(range(VALUES))
            for gr in range(NB) if opening else ():
                order += [("turn", gr, c) for c in range(DT)]
                if gr < NB - 1:
                    order += [("value", next(values), 0) for _ in range(4)]
            order += [("chunk", 0, c) for c in range(NB)]
            maxima = iter([(blk, kt) for blk in range(2) for kt in range(KT)])
            rest = list(values)
            for k in rest:
                order.append(("value", k, 0))
                if k >= rest[0] + 8:
                    order += [("max", *next(maxima)) for _ in range(2 if opening else 1)]
            left = list(maxima)
            for c in range(NB):
                order.append(("chunk", 1, c))
                order += [("max", *m) for m in left[c * len(left) // NB:(c + 1) * len(left) // NB]]
            count = {True: 0, False: 0}
            for kind, a, b in order:
                on_side = kind in ("chunk", "max")
                yield kind, a, b, count[on_side]
                count[on_side] += 1
            assert count == {True: PRO_AUX, False: VALUES + (TURNS if opening else 0)}

        def norm_at(t):
            k, rest = divmod(t - 2 * KT, 7)
            return k if rest == 0 and 0 <= k < NB else None

        def side_items(u, last, coming, n):
            maxima, chunks, turns = ([[] for _ in range(STEPS)] for _ in range(3))
            for t in range(STEPS):
                j, kt = divmod(t, KT)
                ahead = 0 if j < NB - 2 else 1
                if not (last and u == 1 and ahead):
                    maxima[t].append((ahead, (j + 2) % NB, kt, n))
                    n += 1
                if not last and ahead and kt in CHUNKS_AT:
                    chunks[t].append((2 * (j - NB + 2) + CHUNKS_AT.index(kt), n))
                    n += 1
                if coming and u == 1 and norm_at(t - 4) is not None:
                    for c in range(DT):
                        turns[t].append((norm_at(t - 4), c, n))
                        n += 1
            return maxima, chunks, turns, n

        def walk(eng, prologue, head):
            def batch(b, more):
                def pair(i, first, last):
                    g = snap(eng, b * H + i)
                    n = 0
                    for u in range(2):
                        n = head(b, i, g, u, first, last, more and last, n)

                pair(0, True, False)
                with eng.Fori(1, HH - 1) as k:
                    pair(eng.snap(k * 2), False, False)
                pair(H - 2, False, True)

            prologue(0, True)
            with eng.Fori(0, B - 1) as b:
                batch(b, True)
                prologue(snap(eng, b + 1), False)
            batch(B - 1, False)

        block = ctx.enter_context(nc.Block())

        @block.sync
        def _(sp):
            sp.sem_inc(slot_full, 16)
            for u in range(2):
                sp.sem_inc(max_row[u], 16)
                sp.sem_inc(ctx_out[u], 16)
            for k in range(4):
                sp.sem_inc(v_kept[k], 16)
            sp.dma_start(ident[:, :], ident_in).then_inc(const_in, 16)
            sp.dma_start(bias[:, :], bqk).then_inc(const_in, 16)

            def load_w(hd, g):
                sp.wait_ge(w_split, g + 1)
                sp.dma_start(w_raw[:, :, :], wqk_src[bass.ds(hd, 1)]).then_inc(w_in, 16)

            def fill(u, g):
                sp.wait_ge(staged, (g + 1) * NB + 1)
                for dst, src in ((qA[u][0:K], hi_st[0:K]), (qA[u][K:P], lo_st[0:K]),
                                 (kA[u][0:K], hi_st[K:P]), (kA[u][K:P], hi_st[K:P]),
                                 (qB[u][0:K], hi_st[0:K]), (kB[u][0:K], lo_st[K:P])):
                    sp.dma_start(dst.bitcast(F32), src).then_inc(slot_full, 16)

            def load_x(b):
                for k in range(NB):
                    sp.dma_start(x_all[:, k], x_src[bass.ds(b, 1), k]).then_inc(x_in[k], 16)

            def load_v(b, hd, u):
                sp.dma_start(V[u][:, :, :], v_scratch[bass.ds(b, 1), bass.ds(hd, 1)]).then_inc(v_full[u], 16)

            def max_row_in(u, blk, n):
                sp.wait_ge(negm_ready, n + 1)
                dst = qB[u][K:K + 1, blk * BLK:(blk + 1) * BLK].rearrange("o (p t) -> o p t", t=TB)
                sp.dma_start(dst.bitcast(F32), negm[:, blk % 2, :].bitcast(F32)).then_inc(max_row[blk % 2], 16)

            def prologue(b, opening):
                g = snap(sp, b * H)
                if opening:
                    load_x(b)
                    load_w(0, g)
                sp.wait_ge(pv_done, g * STEPS + PROBS)
                sp.dma_start(wv_raw, wv_src).then_inc(wv_in, 16)
                sp.dma_start(bv_all, bv.rearrange("(o n) -> o n", o=1).to_broadcast([P, H * K])).then_inc(bv_in, 16)
                for kind, a, c, _ in prologue_items(opening):
                    if kind == "value":
                        sp.wait_ge(v_ready, b * KT * 2 + a + 1)
                        sp.dma_start(v_dst[bass.ds(b, 1), a % 2, a // 2], v_new[:, a % 4]).then_inc(v_kept[a % 4], 16)
                    elif kind == "chunk" and a == 0 and c == NB - 1:
                        fill(0, g)
                        load_w(1, g + 1)
                max_row_in(0, 0, g * NB)
                for k in range(4):
                    sp.wait_ge(v_kept[k], b * KT * 8 + KT * 8 + 16)
                load_v(b, 0, 0)
                max_row_in(0, 1, g * NB + 1)

            def load_for_feed_forward():
                for u in range(2):
                    sp.wait_ge(ctx_out[u], H * NB // 2 * 16 + 16)
                sp.wait_ge(slot_full, B * H * 96 + 16)
                sp.dma_start(c_first, c_src)\
                    .then_inc(c_loaded, 16)
                sp.dma_start(hi_st[:, :].rearrange("p (c n) -> p c n", n=D), Wo.rearrange("(c p) n -> p c n", p=P))\
                    .then_inc(wo_loaded, 16)

            def head(b, i, g, u, first, last, coming, n):
                if last and u == 1 and not coming:
                    load_for_feed_forward()
                if not (last and u == 1):
                    sp.wait_ge(pv_done, (g + u) * STEPS + PROBS)
                    fill(1 - u, g + u + 1)
                    load_v(b, i + u + 1, 1 - u)
                if not last:
                    load_w(i + u + 2, g + u + 2)
                elif coming and u == 0:
                    load_w(0, g + 2)
                    load_x(b + 1)
                for j in range(NB):
                    ahead = 0 if j < NB - 2 else 1
                    if not (last and u == 1 and ahead):
                        max_row_in((u + ahead) % 2, (j + 2) % NB, (g + u) * NB + j + 2)
                    sp.wait_ge(ctx_ready, (g + u) * NB + j + 1)
                    sp.dma_start(out_dst[bass.ds(b, 1), bass.ds(i + u, 1), j],
                                 ctx_n[:, j % 2]).then_inc(ctx_out[j % 2], 16)
                return n

            walk(sp, prologue, head)
            for u in range(2):
                sp.wait_ge(ctx_out[u], (B * H * NB // 2 + 1) * 16)

        @block.gpsimd
        def _(pool):
            pool.sem_inc(staged, 1)
            for u in range(2):
                nc.gpsimd.memset(kB[u][K:K + 1, :].bitcast(F32), 1.0).then_inc(ones_set, 1)
                pool.wait_ge(ones_set, u + 1)

            def low_chunk(g, chunk):
                pool.wait_ge(hi_ready, g * NB + chunk + 1)
                cols = slice(chunk * BLK, (chunk + 1) * BLK)
                nc.gpsimd.tensor_tensor(lo_w[:, cols], qk_new[:, :], hi_st[:, cols], ALU.subtract)\
                    .then_inc(staged, 1)

            def prologue(b, opening):
                for kind, a, c, _ in prologue_items(opening):
                    if kind == "value":
                        vf = p_f[:, 2 + a % 4].rearrange("p (h k) -> p h k", k=K)
                        pool.wait_ge(vh_ready, b * KT * 2 + a + 1)
                        nc.gpsimd.tensor_tensor(vf, vf, v_new[:, a % 4, :, 0:K], ALU.subtract).then_inc(vd_ready, 1)
                    elif kind == "chunk":
                        low_chunk(b * H + a, c)

            def head(b, i, g, u, first, last, coming, n):
                _, chunks, turns, n = side_items(u, last, coming, n)
                for t in range(STEPS):
                    if not lo_on_dve(t):
                        r = t % PROBS
                        pool.wait_ge(exp_done, (g + u) * STEPS + t + 1 + RING)
                        nc.gpsimd.tensor_tensor(p_l[:, r], p_f[:, r], p_h[:, r], ALU.subtract).then_inc(lo_pool, 1)
                    for chunk, _ in chunks[t - AHEAD] if t >= AHEAD else ():
                        low_chunk(g + u + 2, chunk)
                return n

            walk(pool, prologue, head)

        @block.scalar
        def _(act):
            act.sem_inc(exp_done, RING)
            act.sem_inc(ctx_free, 1)

            def copy_sums(nb):
                act.wait_ge(pv_done, (nb + 1) * KT + PROBS)
                act.wait_ge(ev_step, nb * 2 + 2)
                nc.scalar.activation(sums[:, :, :], ps_ctx[:, :, 0:2 * VW], ACT.Copy).then_inc(ctx_free, 1)

            def take_chunk(g, chunk, n, bank):
                if chunk == 0:
                    act.wait_ge(w_split, g + 2)
                act.wait_ge(staged, g * NB + chunk + 1)
                act.wait_ge(aux_full, n + 1)
                nc.scalar.activation(qk_new[:, :], ps_aux[:, bank], ACT.Identity, bias=b_cur[:, 0:1])\
                    .then_inc(qk_ready, 1)

            def prologue(b, opening):
                g0 = snap(act, b * H)
                a0 = snap(act, g0 * AUX + b * TURNS)

                def high_weights():
                    act.wait_ge(wv_in, b * 16 + 16)
                    nc.scalar.activation(wvh_v, wv_raw, ACT.Copy).then_inc(wvh_ready, 1)

                if opening:
                    high_weights()

                def low_value(k):
                    act.wait_ge(vd_ready, b * KT * 2 + k + 1)
                    vf = p_f[:, 2 + k % 4].rearrange("p (h k) -> p h k", k=K)
                    nc.scalar.activation(v_new[:, k % 4, :, K + 1:VW], vf, ACT.Copy, scale=LO_SCALE)\
                        .then_inc(v_ready, 1)

                before = None
                for kind, a, c, m in prologue_items(opening):
                    if kind == "turn":
                        act.wait_ge(pro_full, score_base(b) + m + 1)
                        nc.scalar.activation(xTh[:, c, a * BLK:(a + 1) * BLK], ps_score[:, m % RING], ACT.Copy)\
                            .then_inc(xh_ready, 1)
                    if kind == "value":
                        if a == 0 and not opening:
                            high_weights()
                        act.wait_ge(pro_free, score_base(b) + m + 1 + RING)
                        act.wait_ge(v_kept[a % 4], b * KT * 8 + a // 4 * 16 + 16)
                        vf = p_f[:, 2 + a % 4].rearrange("p (h k) -> p h k", k=K)
                        nc.scalar.activation(v_new[:, a % 4, :, 0:K], vf, ACT.Copy).then_inc(vh_ready, 1)
                    if kind != "max" and before is not None:
                        low_value(before)
                        before = None
                    if kind == "value":
                        before = a
                    if kind == "chunk":
                        take_chunk(g0 + a, c, a0 + m, m % 2)

            def head(b, i, g, u, first, last, coming, n):
                _, chunks, turns, n = side_items(u, last, coming, n)
                for t in range(STEPS):
                    r, bank = t % PROBS, t % RING
                    act.wait_ge(s_full, (g + u) * STEPS + t + 1)
                    act.wait_ge(pv_done, (g + u) * STEPS + t + 1)
                    nc.scalar.activation(p_f[:, r], ps_score[:, bank], ACT.Exp, scale=K ** -0.5)
                    nc.scalar.activation(p_h[:, r], ps_score[:, bank], ACT.Exp, scale=K ** -0.5).then_inc(exp_done, 1)
                    for chunk, k in chunks[t - AHEAD] if t >= AHEAD else ():
                        take_chunk(g + u + 2, chunk, g * AUX + b * TURNS + PRO_AUX + k, k % 2)
                    for gr, c, k in turns[t - AHEAD] if t >= AHEAD else ():
                        act.wait_ge(aux_full, g * AUX + b * TURNS + PRO_AUX + k + 1)
                        nc.scalar.activation(xTh[:, c, gr * BLK:(gr + 1) * BLK], ps_aux[:, k % 2], ACT.Copy)\
                            .then_inc(xh_ready, 1)
                    if t % KT == SUMS_AT and not (first and u == 0 and t < KT):
                        copy_sums((g + u) * NB + t // KT - 1)
                if last and u == 1:
                    copy_sums((g + u) * NB + NB - 1)
                return n

            walk(act, prologue, head)

        @block.vector
        def _(dve):
            dve.sem_inc(pro_free, RING)
            dve.sem_inc(max_read, 2)
            dve.sem_inc(ev_step, 2)
            dve.sem_inc(w_split, 1)
            nc.vector.memset(v_new[:, :, :, K:K + 1], 1.0)
            dve.wait_ge(const_in, 32)

            def split_w(hd, g):
                dve.wait_ge(staged, g * NB + 1)
                nc.vector.tensor_copy(b_cur[:, :], bias[:, bass.ds(hd, 1)])
                dve.wait_ge(w_in, g * 16 + 16)
                nc.vector.tensor_copy(w_h[:, :, :], w_raw[:, :, :]).then_inc(wh_ready, 1)
                dve.wait_ge(wh_ready, g + 1)
                nc.vector.tensor_tensor(w_l[:, :, :], w_raw[:, :, :], w_h[:, :, :].bitcast(F32),
                                        ALU.subtract).then_inc(w_split, 1)

            def high_chunk(g, chunk):
                cols = slice(chunk * BLK, (chunk + 1) * BLK)
                if chunk == 0:
                    dve.wait_ge(slot_full, g * 96 + 16)
                dve.wait_ge(qk_ready, g * NB + chunk + 1)
                nc.vector.tensor_copy(hi_w[:, cols], qk_new[:, :]).then_inc(hi_ready, 1)

            def maximum(hd, blk, kt, n, m, bank):
                tt, ch = divmod(kt, NB)
                dve.wait_ge(aux_full, n + 1)
                nc.vector.reduce_max(mx[:, blk % 2, tt, ch:ch + 1], ps_aux[:, bank], AX_X).then_inc(max_read, 1)
                if kt == KT - 1:
                    dve.wait_ge(max_read, m + 1 + 2)
                    nc.vector.reduce_max(mrow[:, blk % 2], mx[:, blk % 2], AX_X).then_inc(max_step, 1)

            def negate(hd, blk):
                dve.wait_ge(max_step, hd * NB + blk + 1)
                dve.wait_ge(max_row[blk % 2], (hd * (NB // 2) + blk // 2) * 16 + 16)
                nc.vector.tensor_scalar(negm[:, blk % 2], mrow[:, blk % 2], -1.0, P_SHIFT * K ** 0.5,
                                        ALU.mult, ALU.add).then_inc(negm_ready, 1)

            def low(hd, t):
                if lo_on_dve(t):
                    r = t % PROBS
                    dve.wait_ge(exp_done, hd * STEPS + t + 1 + RING)
                    nc.vector.tensor_tensor(p_l[:, r], p_f[:, r], p_h[:, r], ALU.subtract).then_inc(lo_dve, 1)

            def add_sums(nb):
                dve.wait_ge(ctx_free, nb + 2)
                acc = sums[:, :, :].rearrange("p a (t c) -> p (a t) c", c=VW)
                nc.vector.scalar_tensor_tensor(out=ctx_u[:, :, :], in0=acc[:, :, K + 1:VW], scalar=1.0 / LO_SCALE,
                                               in1=acc[:, :, 0:K], op0=ALU.mult, op1=ALU.add).then_inc(ev_step, 1)
                nc.vector.reciprocal(rden[:, :], acc[:, :, K]).then_inc(ev_step, 1)

            def divide(j, nb):
                dve.wait_ge(ev_step, nb * 2 + 4)
                dve.wait_ge(ctx_out[j % 2], (nb - j) * 8 + j // 2 * 16 + 16)
                nc.vector.tensor_tensor(ctx_n[:, j % 2], ctx_u[:, :, :],
                                        rden[:, :].unsqueeze(2).to_broadcast([P, TB, K]), ALU.mult)\
                    .then_inc(ctx_ready, 1)

            def norm_part(b, k, part):
                at = (b * NB + k) * NORM
                if part == 0:
                    dve.wait_ge(x_in[k], b * 16 + 16)
                    moments(nc, dve, x_all[:, k], small, ln_step, at)
                elif part == 1:
                    newton(nc, dve, EPS_LN, small, ln_step, at + MOMENTS)
                else:
                    apply_root(nc, dve, x_all[:, k], x_all[:, k], small, ln_step, at)
                    nc.vector.tensor_copy(x_mean[:, bass.ds(b * NB + k, 1)], mv[:, :, 0].unsqueeze(1))
                    nc.vector.tensor_copy(x_root[:, bass.ds(b * NB + k, 1)], small[3][:, :].unsqueeze(1))

            def low_x(n, gr, c, bank, read):
                dve.wait_ge(xh_ready, n + 1)
                cols = slice(gr * BLK, (gr + 1) * BLK)
                nc.vector.tensor_tensor(xTl[:, c, cols], bank, xTh[:, c, cols].bitcast(F32),
                                        ALU.subtract).then_inc(read, 1)

            def prologue(b, opening):
                g0 = snap(dve, b * H)
                a0 = snap(dve, g0 * AUX + b * TURNS)

                def low_weights():
                    dve.wait_ge(wvh_ready, b + 1)
                    nc.vector.tensor_tensor(wvl_v, wv_raw, wvh_v.bitcast(F32), ALU.subtract).then_inc(wv_ready, 1)
                    dve.wait_ge(wv_ready, b + 1)
                    dve.wait_ge(bv_in, b * 16 + 16)

                def norm_group(k):
                    for part in range(3):
                        norm_part(b, k, part)

                if opening:
                    norm_group(0)
                    low_weights()
                    split_w(0, g0)
                for kind, a, c, m in prologue_items(opening):
                    if kind == "turn":
                        low_x(b * TURNS + a * DT + c, a, c, ps_score[:, m % RING], pro_free)
                        if c == DT - 1 and a < NB - 1:
                            norm_group(a + 1)
                    if kind == "value":
                        if a == 0 and not opening:
                            low_weights()
                        half = a % 2
                        dve.wait_ge(pro_full, score_base(b) + m + 1)
                        if a >= 4:
                            dve.wait_ge(v_ready, b * KT * 2 + a - 3)
                        nc.vector.tensor_tensor(p_f[:, 2 + a % 4], ps_score[:, m % RING],
                                                bv_all[:, half * BLK:(half + 1) * BLK], ALU.add).then_inc(pro_free, 1)
                        if a == 2 * KT - 12:
                            split_w(1, g0 + 1)
                    if kind == "chunk":
                        high_chunk(g0 + a, c)
                    if kind == "max":
                        maximum(g0, a, c, a0 + m, g0 * STEPS + a * KT + c, m % 2)
                        if c == KT - 1:
                            negate(g0, a)
                for t in range(LO_AHEAD):
                    low(g0, t)

            def head(b, i, g, u, first, last, coming, n):
                maxima, chunks, turns, n = side_items(u, last, coming, n)
                for t in range(STEPS):
                    j, kt = divmod(t, KT)
                    if t + LO_AHEAD < STEPS:
                        low(g + u, t + LO_AHEAD)
                    elif not (last and u == 1):
                        low(g + u + 1, t + LO_AHEAD - STEPS)
                    for ahead, blk, k, number in maxima[t]:
                        maximum(g + u + ahead, blk, k, g * AUX + b * TURNS + PRO_AUX + number,
                                (g + u) * STEPS + 2 * KT + t, number % 2)
                    for chunk, _ in chunks[t - CHUNK_LAG] if t >= CHUNK_LAG else ():
                        high_chunk(g + u + 2, chunk)
                    for part in range(3) if coming and u == 1 else ():
                        k = norm_at(t - part)
                        if k is not None:
                            norm_part(b + 1, k, part)
                    for gr, c, k in turns[t - 3] if t >= 3 else ():
                        low_x((b + 1) * TURNS + gr * DT + c, gr, c, ps_aux[:, k % 2], x_split)
                    block_before = not (first and u == 0 and j == 0)
                    if kt == 2 and block_before:
                        add_sums((g + u) * NB + j - 1)
                    if kt == 4 and block_before:
                        divide((j - 1) % NB, (g + u) * NB + j - 1)
                    if kt == 0 and j > 0 and maxima[t - 1]:
                        ahead, blk, _, _ = maxima[t - 1][0]
                        negate(g + u + ahead, blk)
                    if t == KT + 8 and not last:
                        split_w(i + u + 2, g + u + 2)
                    if t == KT + 8 and coming and u == 0:
                        split_w(0, g + 2)
                if maxima[STEPS - 1]:
                    negate(g + u + 1, 1)
                if last and u == 1:
                    add_sums((g + u) * NB + NB - 1)
                    divide(NB - 1, (g + u) * NB + NB - 1)
                return n

            walk(dve, prologue, head)

        @block.tensor
        def _(pe):
            pe.sem_inc(pv_done, PROBS)
            pe.wait_ge(const_in, 32)
            pe.wait_ge(ones_set, 2)

            used = []

            def after_maxima(m):
                used[:] = [(max_read, m + 1), (max_read, m + 2)]

            def project(g, chunk, bank):
                if chunk == 0:
                    pe.wait_ge(w_split, g + 2)
                pe.wait_ge(*used.pop(0))
                used.append((qk_ready, g * NB + chunk + 1))
                cols = slice(chunk * BLK, (chunk + 1) * BLK)
                parts = [(w, t, c) for c in range(DT) for w, t in ((w_h, xTh), (w_l, xTh), (w_h, xTl))]
                for m, (w, t, c) in enumerate(parts):
                    mm = nc.tensor.matmul(ps_aux[:, bank], w[:, c], t[:, c, cols],
                                          start=(m == 0), stop=(m == len(parts) - 1))
                mm.then_inc(aux_full, 1)

            def max_tile(u, g, blk, kt, m, bank):
                tt, ch = divmod(kt, NB)
                if blk % 2 == 0 and kt == 0:
                    pe.wait_ge(slot_full, g * 96 + 96 + 16)
                pe.wait_ge(*used.pop(0))
                used.append((max_read, m + 3))
                q = qA[u][:, blk * BLK:(blk + 1) * BLK].rearrange("k (p t) -> k t p", t=TB)[:, tt]
                nc.tensor.matmul(ps_aux[:, bank], q, kA[u][:, ch * BLK:(ch + 1) * BLK],
                                 start=True, stop=True).then_inc(aux_full, 1)

            def score(u, g, t):
                j, kt = divmod(t, KT)
                if kt == 0:
                    pe.wait_ge(max_row[j % 2], (g * (NB // 2) + j // 2) * 16 + 32)
                pe.wait_ge(exp_done, g * STEPS + t + 1)
                keys, cols = slice(kt * P, (kt + 1) * P), slice(j * BLK, (j + 1) * BLK)
                nc.tensor.matmul(ps_score[:, t % RING], kA[u][:, keys], qA[u][:, cols], start=True, stop=False)
                nc.tensor.matmul(ps_score[:, t % RING], kB[u][:, keys], qB[u][:, cols],
                                 start=False, stop=True).then_inc(s_full, 1)

            def weigh(u, g, t):
                j, kt = divmod(t, KT)
                r = t % PROBS
                if kt == 0:
                    pe.wait_ge(ctx_free, (g + u) * NB + j + 1)
                if t == 0:
                    pe.wait_ge(v_full[u], g * 8 + 16)
                nd, npl = lo_counts(t)
                if lo_on_dve(t):
                    pe.wait_ge(lo_dve, (g + u) * DVE_LO + nd)
                else:
                    pe.wait_ge(lo_pool, (g + u) * POOL_LO + npl)
                for q in range(TB):
                    acc = ps_ctx[:, q // 2, (q % 2) * VW:(q % 2 + 1) * VW]
                    parts = [(p_h, VW), (p_l, K + 1)]
                    if q % 2:
                        parts.reverse()
                    for p, width in parts:
                        mm = nc.tensor.matmul(acc[:, 0:width], p[:, r, q * P:(q + 1) * P], V[u][:, kt, 0:width],
                                              start=(kt == 0 and q % 2 == 0 and p is p_h),
                                              stop=(kt == KT - 1 and q % 2 == 1 and p is p_h),
                                              skip_group_check=True)
                mm.then_inc(pv_done, 1)

            turned = [m for kind, _, c, m in prologue_items(True) if kind == "turn" and c == DT - 1]

            def prologue(b, opening):
                g0 = snap(pe, b * H)
                if opening:
                    after_maxima(g0 * STEPS)
                else:
                    used[:] = [(x_split, b * TURNS - 1), (x_split, b * TURNS)]
                pe.wait_ge(exp_done, g0 * STEPS + RING)
                for kind, a, c, m in prologue_items(opening):
                    if kind == "turn":
                        if c == 0:
                            pe.wait_ge(ln_step, (b * NB + a + 1) * NORM)
                        pe.wait_ge(pro_free, score_base(b) + m + 1)
                        for t in range(TB):
                            mm = nc.tensor.transpose(ps_score[:, m % RING, t * P:(t + 1) * P],
                                                     x_all[:, a, t, c * P:(c + 1) * P], ident[:, :])
                        mm.then_inc(pro_full, 1)
                    if kind == "value":
                        if a == 0:
                            pe.wait_ge(wv_ready, b + 1)
                        if a % 8 == 0 and opening:
                            pe.wait_ge(pro_free, score_base(b) + turned[a // 8] + 1 + RING)
                        tt, half = divmod(a, 2)
                        pe.wait_ge(pro_free, score_base(b) + m + 1)
                        toks, cols = slice(tt * P, (tt + 1) * P), slice(half * BLK, (half + 1) * BLK)
                        parts = [(t, w, ct) for ct in range(DT)
                                 for t, w in ((xTh, wvh_v), (xTh, wvl_v), (xTl, wvh_v))]
                        for n, (t, w, ct) in enumerate(parts):
                            mm = nc.tensor.matmul(ps_score[:, m % RING], t[:, ct, toks], w[:, ct, cols],
                                                  start=(n == 0), stop=(n == len(parts) - 1))
                        mm.then_inc(pro_full, 1)
                    if kind == "chunk":
                        if a == 0 and c == 0:
                            if opening:
                                pe.wait_ge(pro_free, score_base(b) + turned[-1] + 1 + RING)
                            else:
                                pe.wait_ge(x_split, b * TURNS)
                        project(g0 + a, c, m % 2)
                    if kind == "max":
                        max_tile(0, g0, a, c, g0 * STEPS + a * KT + c, m % 2)
                pe.wait_ge(pro_free, score_base(b) + VALUES + (TURNS if opening else 0) + RING)
                for t in range(AHEAD):
                    score(0, g0, t)

            def head(b, i, g, u, first, last, coming, n):
                maxima, chunks, turns, n = side_items(u, last, coming, n)
                if u == 0:
                    after_maxima(g * STEPS + 2 * KT)
                for t in range(STEPS):
                    j, kt = divmod(t, KT)
                    for ahead, blk, k, number in maxima[t]:
                        max_tile((u + ahead) % 2, g + u + ahead, blk, k, (g + u) * STEPS + 2 * KT + t, number % 2)
                    for gr, c, number in turns[t]:
                        if c == 0:
                            pe.wait_ge(ln_step, ((b + 1) * NB + gr + 1) * NORM)
                        pe.wait_ge(*used.pop(0))
                        used.append((x_split, b * TURNS + gr * DT + c + 1))
                        for k in range(TB):
                            mm = nc.tensor.transpose(ps_aux[:, number % 2, k * P:(k + 1) * P],
                                                     x_all[:, gr, k, c * P:(c + 1) * P], ident[:, :])
                        mm.then_inc(aux_full, 1)
                    if t + AHEAD < STEPS:
                        score(u, g + u, t + AHEAD)
                    elif not (last and u == 1):
                        score(1 - u, g + u + 1, t + AHEAD - STEPS)
                    if t % 2:
                        weigh(u, g, t - 1)
                        for chunk, number in chunks[t]:
                            project(g + u + 2, chunk, number % 2)
                        weigh(u, g, t)
                return n

            walk(pe, prologue, head)


def feed_forward(nc, x, scratch, Wo, bo, gamma, beta, wgT, wuT, wdT, out, shared):
    B, S, D = x.shape
    HK = Wo.shape[0]
    F = wgT.shape[1]
    DT, CT, FT = D // P, HK // P, F // P
    TB = BLK // P
    G = B * S // BLK
    FEED = CT + DT
    TURN = FEED + 2 * DT
    CHAIN = 3 * ROOT + 4
    ident, x_mean, x_root, x_all, stage, c_loaded, wo_loaded = shared
    assert DT == 2 and TB == 4 and CT == 8 and FT % 2 == 0 and FT >= 5 and G % 2 == 0 and G >= 4

    def turn_base(g):
        if isinstance(g, int) and g == G - 1:
            return 2 * FEED + DT + (G - 2) * TURN + 2 * DT
        return g * TURN + 2 * FEED + DT

    def feed_at(f):
        return range(f * CT // FT, (f + 1) * CT // FT)

    with ExitStack() as ctx:
        sb = lambda n, s, d: ctx.enter_context(nc.sbuf_tensor(n, s, d))
        sem = lambda n: ctx.enter_context(nc.semaphore(n))
        bank = lambda n, k: ctx.enter_context(nc.psum_tensor(n, [P, k, BLK], F32))
        ps_t = bank("ps_t", 2)
        ps_y = bank("ps_y", 2)
        ps_g = bank("ps_g", 2)
        ps_u = bank("ps_u", 2)

        bo_c = sb("bo_c", [P, DT], F32)
        gam = sb("gam", [P, D], F32)
        bet = sb("bet", [P, D], F32)
        wo = [sb(f"wo{m}", [P, CT, D], F32R) for m in "hl"]
        wg = [sb(f"wg{m}", [P, DT, F], F32R) for m in "hl"]
        wu = [sb(f"wu{m}", [P, DT, F], F32R) for m in "hl"]
        wd = [sb(f"wd{m}", [P, FT, D], F32R) for m in "hl"]
        c_in = x_all[:, :, :, :].rearrange("p g t d -> p (g t d)").rearrange("p (t n) -> p t n", t=TB)
        x_t = [sb(f"x_t{u}", [P, TB, D], F32) for u in range(2)]
        cT = [sb(f"cT{m}", [P, CT, BLK], F32R) for m in "hl"]
        yT = sb("yT", [P, DT, BLK], F32)
        xn = sb("xn", [P, TB, D], F32)
        z = sb("z", [P, TB, D], F32)
        late = sb("late", [P, 5, TB * D], F32)
        tokens = lambda n: late[:, n].rearrange("p (t d) -> p t d", t=TB)
        halves = lambda n: late[:, n].rearrange("p (c n) -> p c n", c=DT)
        sg, hf, oT = halves(0), halves(1), halves(2)
        o_tok = tokens(3)
        x1 = [sb("x1_0", [P, TB, D], F32), tokens(4)]
        xn2 = sb("xn2", [P, TB, D], F32)
        nT = [sb(f"nT{m}", [P, DT, BLK], F32R) for m in "hl"]
        hT = [sb(f"hT{m}", [P, FT, BLK], F32R) for m in "hl"]
        st2 = sb("st2", [P, TB, 6], F32)
        mv2 = sb("mv2", [P, TB, 2], F32)
        small = (st2, mv2, *(sb(f"norm2_{k}", [P, TB], F32) for k in range(3)))

        const_loaded = sem("const_loaded")
        w_loaded = [wo_loaded] + [sem(f"w_loaded{k}") for k in range(1, 4)]
        w_float = sem("w_float")
        w_hi = sem("w_hi")
        w_parts = sem("w_parts")
        x_loaded = [sem(f"x_loaded{u}") for u in range(2)]
        x_used = sem("x_used")
        centred = sem("centred")
        xn_ready = sem("xn_ready")
        t_full = sem("t_full")
        t_free = sem("t_free")
        c_hi = sem("c_hi")
        y_full = sem("y_full")
        y_read = sem("y_read")
        chain_step = sem("chain_step")
        n_hi = sem("n_hi")
        g_full = sem("g_full")
        silu_done = sem("silu_done")
        u_full = sem("u_full")
        h_ready = sem("h_ready")
        h_hi = sem("h_hi")
        h_lo = sem("h_lo")
        o_full = sem("o_full")
        o_read = sem("o_read")
        end_step = sem("end_step")
        res_ready = sem("res_ready")
        stored = [sem(f"stored{u}") for u in range(2)]

        xv = x.rearrange("b (g t p) d -> (b g) p t d", p=P, t=TB)
        ov = out.rearrange("b (g t p) d -> (b g) p t d", p=P, t=TB)
        cv = scratch.rearrange("b (g t p) n -> (b g) p t n", p=P, t=TB)
        flat = late[:, :, :].rearrange("p a n -> p (a n)")
        cut = lambda a, c, n: flat[:, a:a + c * n].rearrange("p (c n) -> p c n", c=c)
        stage_o = stage[:, :].rearrange("p (c n) -> p c n", c=CT)
        stage_g, stage_u, stage_d = (cut(k * DT * F, c, DT * F // c).bitcast(I32) for k, c in enumerate((DT, DT, FT)))
        assert 3 * DT * F <= 5 * TB * D
        weights = [(Wo.rearrange("(c p) n -> p c n", p=P), stage_o, wo),
                   (wgT.rearrange("(c p) n -> p c n", p=P), stage_g, wg),
                   (wuT.rearrange("(c p) n -> p c n", p=P), stage_u, wu),
                   (wdT.rearrange("(c p) n -> p c n", p=P), stage_d, wd)]

        def walk(eng, feed, chain, turn, end):
            feed(0, 0)
            feed(1, 1)
            chain(0, 0)
            turn(0, 0, True, True, True)
            with eng.Fori(0, (G - 4) // 2) as i:
                g = eng.snap(i * 2 + 1)
                turn(g, 1, False, True, True)
                turn(g + 1, 0, False, True, True)
            turn(G - 3, 1, False, True, True)
            turn(G - 2, 0, False, False, True)
            turn(G - 1, 1, False, False, False)
            end(G - 1, 1)

        nothing = lambda g, u: None
        block = ctx.enter_context(nc.Block())

        @block.sync
        def _(sp):
            row = lambda v: v.rearrange("(o n) -> o n", o=1).to_broadcast([P, D])

            def load_c(g, transposed):
                sp.wait_ge(t_full, transposed)
                sp.dma_start(c_in, cv[bass.ds(g, 1)]).then_inc(c_loaded, 16)

            def load_x(g, u):
                sp.wait_ge(x_used, g + 1)
                sp.dma_start(x_t[u][:, :, :], xv[bass.ds(g, 1)]).then_inc(x_loaded[u], 16)

            def load_w(k):
                src, stage, _ = weights[k]
                sp.dma_start(stage, src).then_inc(w_loaded[k], 16)

            def store(g, u):
                sp.wait_ge(res_ready, g + 2)
                sp.dma_start(ov[bass.ds(g, 1)], x1[u][:, :, :]).then_inc(stored[u], 16)

            for u in range(2):
                sp.sem_inc(stored[u], 16)
            sp.dma_start(bo_c[:, :], bo).then_inc(const_loaded, 16)
            sp.dma_start(gam[:, :], row(gamma)).then_inc(const_loaded, 16)
            sp.dma_start(bet[:, :], row(beta)).then_inc(const_loaded, 16)
            load_x(0, 0)
            load_x(1, 1)
            load_c(1, CT)
            for k in range(1, 4):
                load_w(k)
            load_c(2, FEED + CT)
            load_x(2, 0)

            def turn(g, u, first, feeds, chains):
                if not first:
                    store(g - 1, 1 - u)
                if feeds and not (isinstance(g, int) and g == G - 3):
                    load_c(g + 3, turn_base(g) + CT)
                    load_x(g + 3, 1 - u)

            walk(sp, nothing, nothing, turn, store)
            for u in range(2):
                sp.wait_ge(stored[u], 16 * (G // 2 + 1))

        @block.scalar
        def _(act):
            act.sem_inc(o_read, 3 * DT)
            act.sem_inc(silu_done, 2)

            def hi_c(g, k, item):
                act.wait_ge(t_full, item + 1)
                nc.scalar.activation(cT[0][:, k], ps_t[:, k % 2], ACT.Copy).then_inc(c_hi, 1)

            def copy_y(g):
                for c in range(DT):
                    act.wait_ge(y_full, g * DT + c + 1)
                    nc.scalar.activation(yT[:, c], ps_y[:, c], ACT.Identity, bias=bo_c[:, c:c + 1])\
                        .then_inc(y_read, 1)

            def prepare(k):
                _, stage, parts = weights[k]
                act.wait_ge(w_loaded[k], 16)
                if k:
                    nc.scalar.activation(stage.bitcast(F32), stage, ACT.Copy, scale=1.0 / 127.0).then_inc(w_float, 1)
                    act.wait_ge(w_float, k)
                nc.scalar.activation(parts[0][:, :, :], stage.bitcast(F32) if k else stage, ACT.Copy).then_inc(w_hi, 1)

            def feed(g, u):
                if g == 0:
                    prepare(0)
                for k in range(CT):
                    hi_c(g, k, g * FEED + k)
                if g == 0:
                    act.wait_ge(const_loaded, 48)
                copy_y(g)
                if g == 0:
                    for k in range(1, 4):
                        prepare(k)

            def high_normed(g, item):
                for c in range(DT):
                    act.wait_ge(t_full, item + c + 1)
                    nc.scalar.activation(nT[0][:, c], ps_t[:, c], ACT.Copy).then_inc(n_hi, 1)

            def turn(g, u, first, feeds, chains):
                base = turn_base(g)
                if first:
                    high_normed(g, base - DT)

                def hi_h(f):
                    act.wait_ge(h_ready, g * FT + f + 3)
                    nc.scalar.activation(hT[0][:, f], hf[:, f % 2], ACT.Copy).then_inc(h_hi, 1)

                act.wait_ge(o_full, g * DT + DT)
                for f in range(FT):
                    act.wait_ge(g_full, g * FT + f + 1)
                    act.wait_ge(h_ready, g * FT + f + 1)
                    nc.scalar.activation(sg[:, f % 2], ps_g[:, f % 2], ACT.Silu).then_inc(silu_done, 1)
                    if feeds:
                        for k in feed_at(f):
                            hi_c(g + 2, k, base + k)
                    if f:
                        hi_h(f - 1)
                hi_h(FT - 1)
                if feeds:
                    copy_y(g + 2)
                for c in range(DT):
                    act.wait_ge(o_full, g * DT + c + 1 + DT)
                    nc.scalar.activation(oT[:, c], ps_y[:, c], ACT.Copy).then_inc(o_read, 1)
                if chains:
                    high_normed(g + 1, base + (FEED if feeds else 0))

            walk(act, feed, nothing, turn, nothing)

        @block.gpsimd
        def _(pool):
            pool.sem_inc(h_lo, 2)
            pool.sem_inc(res_ready, 1)

            def norm_x(g, u):
                if not (isinstance(g, int) and g == 0):
                    pool.wait_ge(chain_step, (g - 1) * CHAIN + 1)
                pool.wait_ge(x_loaded[u], (g - u) * 8 + 16)
                stat = lambda v: v[:, bass.ds(g, 1)].rearrange("p o t -> p (o t)").unsqueeze(2)\
                    .to_broadcast([P, TB, D])
                nc.gpsimd.tensor_tensor(xn[:, :, :], x_t[u][:, :, :], stat(x_mean), ALU.subtract)\
                    .then_inc(centred, 1)
                pool.wait_ge(centred, g + 1)
                nc.gpsimd.tensor_tensor(xn[:, :, :], xn[:, :, :], stat(x_root), ALU.mult).then_inc(xn_ready, 1)

            def residual(g, u):
                pool.wait_ge(end_step, (g + 1) * NORM)
                nc.gpsimd.tensor_tensor(x1[u][:, :, :], x1[u][:, :, :], o_tok[:, :, :], ALU.add)\
                    .then_inc(res_ready, 1)

            def turn(g, u, first, feeds, chains):
                for f in range(FT):
                    pool.wait_ge(h_hi, g * FT + f + 1)
                    nc.gpsimd.tensor_tensor(hT[1][:, f], hf[:, f % 2], hT[0][:, f].bitcast(F32),
                                            ALU.subtract).then_inc(h_lo, 1)
                    if f == 1 and not first:
                        residual(g - 1, 1 - u)
                if feeds:
                    norm_x(g + 2, u)

            walk(pool, norm_x, nothing, turn, residual)

        @block.vector
        def _(dve):
            dve.sem_inc(t_free, 2)
            dve.sem_inc(h_ready, 2)
            dve.sem_inc(x_used, 2)
            def prepare(k):
                _, stage, parts = weights[k]
                dve.wait_ge(w_hi, k + 1)
                nc.vector.tensor_tensor(parts[1][:, :, :], stage.bitcast(F32) if k else stage, parts[0][:, :, :].bitcast(F32),
                                        ALU.subtract).then_inc(w_parts, 1)

            def lo_c(g, k):
                dve.wait_ge(c_hi, g * CT + k + 1)
                nc.vector.tensor_tensor(cT[1][:, k], ps_t[:, k % 2], cT[0][:, k].bitcast(F32),
                                        ALU.subtract).then_inc(t_free, 1)

            def add_x(g, item):
                dve.wait_ge(xn_ready, g + 1)
                for c in range(2):
                    dve.wait_ge(t_full, item + c + 1)
                    half = slice(2 * c, 2 * c + 2)
                    nc.vector.tensor_tensor(z[:, half], ps_t[:, c].rearrange("p (t d) -> p t d", d=D), xn[:, half],
                                            ALU.add).then_inc(t_free, 1)
                dve.wait_ge(t_free, item + 2 + 2)

            _, mv, _, y, _ = small
            col = lambda t: (mv[:, t, 0:1], y[:, t:t + 1])

            def moments_z(g, u):
                moments(nc, dve, z, small, chain_step, g * CHAIN)

            def newton_z(g, u):
                newton(nc, dve, EPS_ATTN, small, chain_step, g * CHAIN + MOMENTS)

            def gamma_beta(g, u):
                for t in range(TB):
                    ins = nc.vector.scalar_tensor_tensor(out=z[:, t], in0=z[:, t], scalar=col(t)[0], in1=gam[:, :],
                                                         op0=ALU.subtract, op1=ALU.mult)
                ins.then_inc(chain_step, 1)
                dve.wait_ge(chain_step, g * CHAIN + ROOT + 1)
                for t in range(TB):
                    ins = nc.vector.scalar_tensor_tensor(out=z[:, t], in0=z[:, t], scalar=col(t)[1], in1=bet[:, :],
                                                         op0=ALU.mult, op1=ALU.add)
                ins.then_inc(chain_step, 1)
                dve.wait_ge(chain_step, g * CHAIN + ROOT + 2)

            def root_again(g, u):
                moments(nc, dve, z, small, chain_step, g * CHAIN + ROOT + 2)
                newton(nc, dve, EPS_LN, small, chain_step, g * CHAIN + ROOT + 2 + MOMENTS)

            def first_residual(g, u):
                for t in range(TB):
                    ins = nc.vector.tensor_scalar(z[:, t], z[:, t], *col(t), ALU.subtract, ALU.mult)
                ins.then_inc(chain_step, 1)
                dve.wait_ge(chain_step, g * CHAIN + 2 * ROOT + 3)
                dve.wait_ge(stored[u], (g - u) * 8 + 16)
                nc.vector.tensor_tensor(x1[u][:, :, :], x_t[u][:, :, :], z[:, :, :], ALU.add).then_inc(x_used, 1)
                dve.wait_ge(x_used, g + 3)

            def norm_x1(g, u):
                norm(nc, dve, xn2, x1[u], EPS_LN, small, chain_step, g * CHAIN + 2 * ROOT + 3)

            def last_norm(g, u):
                norm(nc, dve, o_tok, o_tok, EPS_LN, small, end_step, g * NORM)

            def last_moments(g, u):
                moments(nc, dve, o_tok, small, end_step, g * NORM)

            def last_scale(g, u):
                scale(nc, dve, o_tok, o_tok, EPS_LN, small, end_step, g * NORM)

            def feed(g, u):
                if g == 0:
                    prepare(0)
                for k in range(CT):
                    lo_c(g, k)
                    if g == 1 and k in (1, 3, 5):
                        prepare((k + 1) // 2)
                if g == 0:
                    add_x(0, CT)
                    dve.wait_ge(const_loaded, 48)
                    for piece in (moments_z, newton_z, gamma_beta):
                        piece(0, 0)

            def chain(g, u):
                for piece in (root_again, first_residual, norm_x1):
                    piece(g, u)
                add_x(1, FEED + CT)

            def low_normed(g):
                for c in range(DT):
                    dve.wait_ge(n_hi, g * DT + c + 1)
                    nc.vector.tensor_tensor(nT[1][:, c], ps_t[:, c], nT[0][:, c].bitcast(F32),
                                            ALU.subtract).then_inc(t_free, 1)

            def turn(g, u, first, feeds, chains):
                base = turn_base(g)
                if first:
                    low_normed(g)
                for f in range(FT):
                    dve.wait_ge(u_full, g * FT + f + 1)
                    dve.wait_ge(silu_done, g * FT + f + 3)
                    dve.wait_ge(h_lo, g * FT + f + 1)
                    nc.vector.tensor_tensor(hf[:, f % 2], ps_u[:, f % 2], sg[:, f % 2], ALU.mult)\
                        .then_inc(h_ready, 1)
                    if feeds:
                        for k in feed_at(f):
                            lo_c(g + 2, k)
                    if f < 2 and not first:
                        (last_moments, last_scale)[f](g - 1, 1 - u)
                    if 2 <= f < 5 and chains:
                        (moments_z, newton_z, gamma_beta)[f - 2](g + 1, 1 - u)
                if chains:
                    root_again(g + 1, 1 - u)
                    first_residual(g + 1, 1 - u)
                    norm_x1(g + 1, 1 - u)
                item = base
                if feeds:
                    add_x(g + 2, base + CT)
                    item = base + FEED
                if chains:
                    low_normed(g + 1)
                    item = item + DT
                dve.wait_ge(res_ready, g + 1)
                for c in range(2):
                    dve.wait_ge(t_full, item + c + 1)
                    nc.vector.tensor_copy(o_tok[:, 2 * c:2 * c + 2],
                                          ps_t[:, c].rearrange("p (t d) -> p t d", d=D)).then_inc(t_free, 1)
                dve.wait_ge(t_free, item + DT + 2)

            walk(dve, feed, chain, turn, last_norm)

        @block.tensor
        def _(pe):
            pe.sem_inc(o_full, DT)

            def product(dst, terms, ready=None):
                passes = [(w[m], t[k]) for w, t in terms for m, k in ((0, 0), (1, 0), (0, 1))]
                for n, (w, t) in enumerate(passes):
                    if ready is not None and n % 3 == 0:
                        pe.wait_ge(ready[0], ready[1] + n // 3)
                    mm = nc.tensor.matmul(dst, w, t, start=(n == 0), stop=(n == len(passes) - 1))
                return mm

            def turn_back(src, item):
                for c in range(2):
                    pe.wait_ge(t_free, item + c + 1)
                    for t in range(2):
                        for w in range(DT):
                            mm = nc.tensor.transpose(ps_t[:, c, (t * DT + w) * P:(t * DT + w + 1) * P],
                                                     src[:, w, (2 * c + t) * P:(2 * c + t + 1) * P], ident[:, :])
                    mm.then_inc(t_full, 1)

            def turn_tile(bank_of, src, item):
                pe.wait_ge(t_free, item + 1)
                for t in range(TB):
                    mm = nc.tensor.transpose(ps_t[:, bank_of, t * P:(t + 1) * P], src(t), ident[:, :])
                mm.then_inc(t_full, 1)

            def turn_c(k, item):
                turn_tile(k % 2, lambda t: c_in[:, t, k * P:(k + 1) * P], item)

            def project_out(g, item):
                for c in range(DT):
                    pe.wait_ge(o_read, g * DT + c + 1)
                    product(ps_y[:, c], [([w[:, k, c * P:(c + 1) * P] for w in wo], [t[:, k] for t in cT])
                                         for k in range(CT)],
                            ready=(t_free, item + 1 + 2) if c == 0 else None).then_inc(y_full, 1)

            def feed(g, u):
                pe.wait_ge(c_loaded, g * 16 + 16)
                for k in range(CT):
                    turn_c(k, g * FEED + k)
                if g == 0:
                    pe.wait_ge(w_parts, 1)
                project_out(g, g * FEED)
                pe.wait_ge(y_read, g * DT + DT)
                turn_back(yT, g * FEED + CT)

            def turn_normed(g, item):
                pe.wait_ge(chain_step, (g + 1) * CHAIN)
                for c in range(DT):
                    turn_tile(c, lambda t: xn2[:, t, c * P:(c + 1) * P], item + c)

            def turn(g, u, first, feeds, chains):
                base = turn_base(g)
                if first:
                    turn_normed(g, base - DT)
                    pe.wait_ge(w_parts, 4)
                    pe.wait_ge(t_free, base + 2)
                if feeds:
                    pe.wait_ge(c_loaded, (g + 2) * 16 + 16)
                for f in range(FT):
                    fs = slice(f * P, (f + 1) * P)
                    for ps, w, full, free in ((ps_g, wg, g_full, silu_done), (ps_u, wu, u_full, h_ready)):
                        pe.wait_ge(free, g * FT + f + 1)
                        product(ps[:, f % 2], [([v[:, c, fs] for v in w], [t[:, c] for t in nT])
                                               for c in range(DT)]).then_inc(full, 1)
                    if feeds:
                        for k in feed_at(f):
                            turn_c(k, base + k)
                item = base
                if feeds:
                    item = base + CT
                    project_out(g + 2, base)
                for c in range(DT):
                    pe.wait_ge(y_read, (g + 2) * DT + c + 1 if feeds else G * DT)
                    if feeds and c == 1:
                        turn_back(yT, item)
                        item = item + DT
                    if not feeds and not chains:
                        pe.wait_ge(o_read, g * DT + c + 1 + 2 * DT)
                    product(ps_y[:, c], [([w[:, f, c * P:(c + 1) * P] for w in wd], [t[:, f] for t in hT])
                                         for f in range(FT)],
                            ready=(h_lo, g * FT + 1 + 2) if c == 0 else None).then_inc(o_full, 1)
                if chains:
                    turn_normed(g + 1, item)
                    item = item + DT
                pe.wait_ge(o_read, (g + 4) * DT)
                turn_back(oT, item)

            walk(pe, feed, nothing, turn, nothing)


def program(nc, x, wqk, bqk, Wv, bv, Wo, bo, gamma, beta, wgT, wuT, wdT, ident, out):
    B, S, _ = x.shape
    scratch = nc.dram_tensor("heads", (B, S, Wo.shape[0]), F32, kind="Internal").ap()
    v_scratch = nc.dram_tensor("v_heads", (B, wqk.shape[1], P, S // P, wqk.shape[2] + 1), F16, kind="Internal").ap()
    nc.disable_value_cache = True
    groups, tiles = B * S // BLK, BLK // P
    with ExitStack() as ctx:
        sb = lambda n, shape: ctx.enter_context(nc.sbuf_tensor(n, shape, F32))
        shared = (sb("identity", [P, P]), sb("x_mean", [P, groups, tiles]), sb("x_root", [P, groups, tiles]),
                  sb("x_all", [P, S // BLK, tiles, x.shape[2]]),
                  sb("hi_st", [P, S]),
                  ctx.enter_context(nc.semaphore("c_loaded")),
                  ctx.enter_context(nc.semaphore("wo_loaded")))
        attention(nc, x, wqk, bqk, Wv, bv, ident, v_scratch, scratch, Wo, shared)
        feed_forward(nc, x, scratch, Wo, bo, gamma, beta, wgT, wuT, wdT, out, shared)


def kernel(L0_attn_x, L0_attn_Wq, L0_attn_bq, L0_attn_Wk, L0_attn_bk, L0_attn_Wv, L0_attn_bv, L0_attn_Wo,
           L0_attn_bo, L0_attn_gamma, L0_attn_beta, L0_ffn_w_gate, L0_ffn_w_up, L0_ffn_w_down):
    import numpy as np
    import concourse.bacc as bacc
    from concourse.bass_utils import run_bass_kernel_spmd

    a = lambda v: np.ascontiguousarray(v)
    D, H, K = L0_attn_Wq.shape
    arrays = {
        "x": a(L0_attn_x),
        "wqk": a(np.concatenate([L0_attn_Wq, L0_attn_Wk], axis=2)),
        "bqk": a(np.concatenate([L0_attn_bq, L0_attn_bk], axis=1).T),
        "Wv": a(np.reshape(L0_attn_Wv, (D, H * K))),
        "bv": a(np.reshape(L0_attn_bv, (H * K,))),
        "Wo": a(np.reshape(L0_attn_Wo, (H * K, D))),
        "bo": a(np.reshape(L0_attn_bo, (D // P, P)).T),
        "gamma": a(L0_attn_gamma),
        "beta": a(L0_attn_beta),
        "wgT": a(np.transpose(L0_ffn_w_gate)),
        "wuT": a(np.transpose(L0_ffn_w_up)),
        "wdT": a(np.transpose(L0_ffn_w_down)),
        "ident": np.eye(P, dtype=np.float32),
    }
    nc = bacc.Bacc("TRN2", target_bir_lowering=False, num_devices=1)
    args = [nc.dram_tensor(f"in_{n}", v.shape, mybir.dt.from_np(v.dtype), kind="ExternalInput").ap()
            for n, v in arrays.items()]
    out = nc.dram_tensor("out", arrays["x"].shape, F32, kind="ExternalOutput").ap()
    program(nc, *args, out)
    r = run_bass_kernel_spmd(nc, [{f"in_{n}": v for n, v in arrays.items()}], core_ids=[0])
    return r.results[0]["out"]
```
